# Optimizing a Trainium2 kernel written in Bass

```python
import numpy as np
import jax
import jax.numpy as jnp

def _softmax(x, axis=-1):
    return jax.nn.softmax(x, axis=axis)

def _gelu(x):
    return jax.nn.gelu(x, approximate=True)

def _silu(x):
    return jax.nn.silu(x)

def _sigmoid(x):
    return jax.nn.sigmoid(x)

def _layernorm(x, axis=-1, eps=1e-05):
    m = jnp.mean(x, axis=axis, keepdims=True)
    v = jnp.var(x, axis=axis, keepdims=True)
    return (x - m) / jnp.sqrt(v + eps)

def _scatter_add(tgt, idx, src, axis=0):
    return tgt.at[idx].add(src)

def _segment_sum(src, seg, n):
    return jax.ops.segment_sum(src, seg, n)
kernel_name = 'mk_gnn_preln_d4_gnn_r64_779751'

def setup_inputs(seed: int=0):
    np.random.seed(seed)
    _w = jnp.asarray

    def _rec_inputs():
        import jax
        import jax.numpy as jnp
        _gk = jax.random.key(seed)
        x = -0.0005121 + 1.001 * jax.random.normal(jax.random.fold_in(_gk, 1), (100000, 64), jnp.float32)
        src = jax.random.randint(jax.random.fold_in(_gk, 2), (50000,), 0, 100000, jnp.int32)
        dst = jnp.minimum((100000 * jax.random.uniform(jax.random.fold_in(_gk, 3), (50000,)) ** 2.0).astype(jnp.int32), 99999)
        _o = jnp.argsort(dst, stable=True)
        src = src[_o]
        dst = dst[_o]
        edge_attr_32 = -9.77346e-05 + 0.999888 * jax.random.normal(jax.random.fold_in(_gk, 12), (50000, 32), jnp.float32)
        edge_type_3 = jax.random.randint(jax.random.fold_in(_gk, 14), (50000,), 0, 3, jnp.int32)
        edge_type_4 = jax.random.randint(jax.random.fold_in(_gk, 15), (50000,), 0, 4, jnp.int32)
        edge_weight = jax.random.uniform(jax.random.fold_in(_gk, 16), (50000,), jnp.float32, 0.0, 0.999998)
        node_type_2 = jax.random.randint(jax.random.fold_in(_gk, 17), (100000,), 0, 2, jnp.int32)
        return (x, src, dst, edge_attr_32, edge_type_3, edge_type_4, edge_weight, node_type_2)
    x, src, dst, edge_attr_32, edge_type_3, edge_type_4, edge_weight, node_type_2 = _rec_inputs()

    def _L0_gnn_setup():
        import jax, jax.numpy as jnp
        import numpy as np
        N_NODES = 50000
        N_EDGES = 15625
        C_FEAT = 64
        key = jax.random.key(seed)
        k1, k2, k3 = jax.random.split(key, 3)
        x = jax.random.normal(k1, (N_NODES, C_FEAT), dtype=jnp.float32)
        g = jax.random.randint(k2, (2, N_EDGES), 0, N_NODES, dtype=jnp.int64)
        ew = jax.random.uniform(k3, (N_EDGES,), dtype=jnp.float32)
        return {'x': x, 'g': g, 'ew': ew}
    _L0_gnn_all = _L0_gnn_setup()
    _L0_gnn_in = {k: v for k, v in _L0_gnn_all.items() if k in ()}
    del _L0_gnn_all

    def _L1_gnn_setup():
        import jax, jax.numpy as jnp
        import numpy as np
        N = 50000
        E = 12500
        H = 64
        K = 4
        STEPS = 4

        def _gru_cell(a, feat, w_ih, w_hh, b_ih, b_hh):
            gi = a @ w_ih.T + b_ih
            gh = feat @ w_hh.T + b_hh
            i_r, i_z, i_n = jnp.split(gi, 3, axis=-1)
            h_r, h_z, h_n = jnp.split(gh, 3, axis=-1)
            r = jax.nn.sigmoid(i_r + h_r)
            z = jax.nn.sigmoid(i_z + h_z)
            n = jnp.tanh(i_n + r * h_n)
            return (1.0 - z) * n + z * feat
        key = jax.random.key(seed)
        ks = jax.random.split(key, 10)
        s = 0.05
        return {'h': jax.random.normal(ks[0], (N, H), jnp.float32), 'W': jax.random.normal(ks[1], (K, H, H), jnp.float32) * s, 'b': jax.random.normal(ks[2], (K, H), jnp.float32) * s, 'w_ih': jax.random.normal(ks[3], (3 * H, H), jnp.float32) * s, 'w_hh': jax.random.normal(ks[4], (3 * H, H), jnp.float32) * s, 'b_ih': jax.random.normal(ks[5], (3 * H,), jnp.float32) * s, 'b_hh': jax.random.normal(ks[6], (3 * H,), jnp.float32) * s, 'src': jax.random.randint(ks[7], (E,), 0, N, dtype=jnp.int32), 'dst': jax.random.randint(ks[8], (E,), 0, N, dtype=jnp.int32), 'etypes': jax.random.randint(ks[9], (E,), 0, K, dtype=jnp.int32)}
    _L1_gnn_all = _L1_gnn_setup()
    _L1_gnn_in = {k: v for k, v in _L1_gnn_all.items() if k in ('W', 'b', 'w_ih', 'w_hh', 'b_ih', 'b_hh')}
    del _L1_gnn_all

    def _L2_gnn_setup():
        import jax, jax.numpy as jnp
        import numpy as np
        N_NODES = 100000
        N_EDGES = 25000
        D_IN = 64
        D_OUT = 64
        E_DIM = 32
        N_NODE_TYPES = 2
        N_EDGE_TYPES = 3
        key = jax.random.key(seed)
        ks = jax.random.split(key, 7)
        node_feature = jax.random.normal(ks[0], (N_NODES, D_IN), dtype=jnp.float32)
        edge_feature = jax.random.normal(ks[1], (N_EDGES, E_DIM), dtype=jnp.float32)
        W_node = jax.random.normal(ks[2], (N_NODE_TYPES, D_IN, D_OUT), dtype=jnp.float32) / np.sqrt(D_IN)
        W_msg = jax.random.normal(ks[3], (N_EDGE_TYPES, D_OUT + E_DIM, D_OUT), dtype=jnp.float32) / np.sqrt(D_OUT + E_DIM)
        node_type = jax.random.randint(ks[4], (N_NODES,), 0, N_NODE_TYPES, dtype=jnp.int32)
        edge_type = jax.random.randint(ks[5], (N_EDGES,), 0, N_EDGE_TYPES, dtype=jnp.int32)
        edge_index = jax.random.randint(ks[6], (2, N_EDGES), 0, N_NODES, dtype=jnp.int32)
        return {'node_feature': node_feature, 'edge_feature': edge_feature, 'W_node': W_node, 'W_msg': W_msg, 'node_type': node_type, 'edge_type': edge_type, 'edge_index': edge_index}
    _L2_gnn_all = _L2_gnn_setup()
    _L2_gnn_in = {k: v for k, v in _L2_gnn_all.items() if k in ('W_node', 'W_msg')}
    del _L2_gnn_all

    def _L3_gnn_setup():
        import jax, jax.numpy as jnp
        import numpy as np
        N_NODES = 50000
        N_EDGES = 12500
        D = 64

        def _leaky_relu(x, slope=0.2):
            return jnp.where(x >= 0, x, slope * x)
        key = jax.random.key(seed)
        ks = jax.random.split(key, 6)
        feats = jax.random.normal(ks[0], (N_NODES, D), dtype=jnp.float32)
        src = jax.random.randint(ks[1], (N_EDGES,), 0, N_NODES, dtype=jnp.int32)
        dst = jax.random.randint(ks[2], (N_EDGES,), 0, N_NODES, dtype=jnp.int32)
        W = jax.random.normal(ks[3], (D, D), dtype=jnp.float32) * (1.0 / np.sqrt(D))
        attn_l = jax.random.normal(ks[4], (D,), dtype=jnp.float32) * (1.0 / np.sqrt(D))
        attn_r = jax.random.normal(ks[5], (D,), dtype=jnp.float32) * (1.0 / np.sqrt(D))
        bias = jnp.zeros((D,), dtype=jnp.float32)
        return {'feats': feats, 'src': src, 'dst': dst, 'W': W, 'attn_l': attn_l, 'attn_r': attn_r, 'bias': bias}
    _L3_gnn_all = _L3_gnn_setup()
    _L3_gnn_in = {k: v for k, v in _L3_gnn_all.items() if k in ('W', 'attn_l', 'attn_r', 'bias')}
    del _L3_gnn_all
    return {'x': x, 'src': src, 'dst': dst, 'edge_attr_32': edge_attr_32, 'edge_type_3': edge_type_3, 'edge_type_4': edge_type_4, 'edge_weight': edge_weight, 'node_type_2': node_type_2, 'L1_gnn_W': _L1_gnn_in['W'], 'L1_gnn_b': _L1_gnn_in['b'], 'L1_gnn_w_ih': _L1_gnn_in['w_ih'], 'L1_gnn_w_hh': _L1_gnn_in['w_hh'], 'L1_gnn_b_ih': _L1_gnn_in['b_ih'], 'L1_gnn_b_hh': _L1_gnn_in['b_hh'], 'L2_gnn_W_node': _L2_gnn_in['W_node'], 'L2_gnn_W_msg': _L2_gnn_in['W_msg'], 'L3_gnn_W': _L3_gnn_in['W'], 'L3_gnn_attn_l': _L3_gnn_in['attn_l'], 'L3_gnn_attn_r': _L3_gnn_in['attn_r'], 'L3_gnn_bias': _L3_gnn_in['bias']}

def reference(x, src, dst, edge_attr_32, edge_type_3, edge_type_4, edge_weight, node_type_2, L1_gnn_W, L1_gnn_b, L1_gnn_w_ih, L1_gnn_w_hh, L1_gnn_b_ih, L1_gnn_b_hh, L2_gnn_W_node, L2_gnn_W_msg, L3_gnn_W, L3_gnn_attn_l, L3_gnn_attn_r, L3_gnn_bias):
    import jax
    import jax.numpy as jnp

    def _L0_gnn_ref(x, g, ew):
        import jax, jax.numpy as jnp
        import numpy as np
        N_NODES = 50000
        N_EDGES = 15625
        C_FEAT = 64
        i, j = (g[0], g[1])
        weighted_info = x[i] * ew[:, None]
        aggr_out = jax.ops.segment_sum(weighted_info, j, num_segments=x.shape[0])
        return aggr_out

    def _L1_gnn_ref(h, W, b, w_ih, w_hh, b_ih, b_hh, src, dst, etypes):
        import jax, jax.numpy as jnp
        import numpy as np
        N = 50000
        E = 12500
        H = 64
        K = 4
        STEPS = 4

        def _gru_cell(a, feat, w_ih, w_hh, b_ih, b_hh):
            gi = a @ w_ih.T + b_ih
            gh = feat @ w_hh.T + b_hh
            i_r, i_z, i_n = jnp.split(gi, 3, axis=-1)
            h_r, h_z, h_n = jnp.split(gh, 3, axis=-1)
            r = jax.nn.sigmoid(i_r + h_r)
            z = jax.nn.sigmoid(i_z + h_z)
            n = jnp.tanh(i_n + r * h_n)
            return (1.0 - z) * n + z * feat
        num_nodes = h.shape[0]

        def step(feat, _):
            transformed = jnp.einsum('nd,khd->knh', feat, W) + b[:, None, :]
            msgs = transformed[etypes, src]
            a = jax.ops.segment_sum(msgs, dst, num_segments=num_nodes)
            feat = _gru_cell(a, feat, w_ih, w_hh, b_ih, b_hh)
            return (feat, None)
        feat, _ = jax.lax.scan(step, h, None, length=STEPS)
        return feat

    def _L2_gnn_ref(node_feature, edge_feature, W_node, W_msg, node_type, edge_type, edge_index):
        import jax, jax.numpy as jnp
        import numpy as np
        N_NODES = 100000
        N_EDGES = 25000
        D_IN = 64
        D_OUT = 64
        E_DIM = 32
        N_NODE_TYPES = 2
        N_EDGE_TYPES = 3
        x_out = jnp.zeros((node_feature.shape[0], W_node.shape[2]), dtype=node_feature.dtype)
        for t in range(W_node.shape[0]):
            x_out = x_out + jnp.where((node_type == t)[:, None], node_feature @ W_node[t], 0.0)
        src, dst = (edge_index[0], edge_index[1])
        x_cat = jnp.concatenate([x_out[src], edge_feature], axis=-1)
        msg = jnp.zeros((x_cat.shape[0], W_msg.shape[2]), dtype=x_cat.dtype)
        for t in range(W_msg.shape[0]):
            msg = msg + jnp.where((edge_type == t)[:, None], x_cat @ W_msg[t], 0.0)
        out = jax.ops.segment_sum(msg, dst, num_segments=node_feature.shape[0])
        return out

    def _L3_gnn_ref(feats, src, dst, W, attn_l, attn_r, bias):
        import jax, jax.numpy as jnp
        import numpy as np
        N_NODES = 50000
        N_EDGES = 12500
        D = 64

        def _leaky_relu(x, slope=0.2):
            return jnp.where(x >= 0, x, slope * x)
        n = feats.shape[0]
        h = _leaky_relu(feats)
        z = h @ W
        el = z @ attn_l
        er = z @ attn_r
        e = _leaky_relu(el[src] + er[dst])
        emax = jax.ops.segment_max(e, dst, num_segments=n)
        emax = jnp.where(jnp.isfinite(emax), emax, 0.0)
        ex = jnp.exp(e - emax[dst])
        denom = jax.ops.segment_sum(ex, dst, num_segments=n)
        denom = jnp.where(denom == 0, 1.0, denom)
        alpha = ex / denom[dst]
        msg = alpha[:, None] * z[src]
        rst = jax.ops.segment_sum(msg, dst, num_segments=n)
        return rst + bias
    edge_index = jnp.stack([src, dst])
    h = jnp.maximum(_layernorm(x, axis=-1), 0.0)
    x = x + _L0_gnn_ref(h, edge_index, edge_weight)
    h = jnp.maximum(_layernorm(x, axis=-1), 0.0)
    x = x + _L1_gnn_ref(h, L1_gnn_W, L1_gnn_b, L1_gnn_w_ih, L1_gnn_w_hh, L1_gnn_b_ih, L1_gnn_b_hh, src, dst, edge_type_4)
    h = jnp.maximum(_layernorm(x, axis=-1), 0.0)
    x = x + _L2_gnn_ref(h, edge_attr_32, L2_gnn_W_node, L2_gnn_W_msg, node_type_2, edge_type_3, edge_index)
    h = jnp.maximum(_layernorm(x, axis=-1), 0.0)
    x = x + _L3_gnn_ref(h, src, dst, L3_gnn_W, L3_gnn_attn_l, L3_gnn_attn_r, L3_gnn_bias)
    return x

_drawn_inputs = setup_inputs


def setup_inputs(seed=0):
    import zlib

    import numpy as np

    out = dict(_drawn_inputs(seed))
    spreads = {'L3_gnn_bias': (0.0, 0.1)}
    factors = {'L1_gnn_b': 3.985, 'L1_gnn_b_hh': 2.799, 'L3_gnn_attn_r': 6.418}
    for name, (base, spread) in spreads.items():
        noise = np.random.default_rng([zlib.crc32(name.encode()), seed]).standard_normal(out[name].shape)
        drawn = base * np.exp(spread * noise) if base else spread * noise
        out[name] = jnp.asarray(drawn.astype(out[name].dtype))
    for name, factor in factors.items():
        out[name] = (out[name] * factor).astype(out[name].dtype)
    return out
```

```python
from contextlib import ExitStack

import concourse.bass as bass
from concourse import mybir

F32 = mybir.dt.float32
BF16 = mybir.dt.bfloat16
I32 = mybir.dt.int32
ALU = mybir.AluOpType
ACT = mybir.ActivationFunctionType
AX = mybir.AxisListType

P = 128
D = 64
N = 100000
E = 50000
U = 7
T = 392
NG = T // U
EP = T * P
FRONT = 2 * U
CH = 4
R = T // CH
GD = 8
ND = 98
NP_ = ND * GD * P
FAR = float(1 << 20)
BIG = 1e30
EPS = 1e-5
RING = 2


def tile_base(n):
    return T - U * (n + 1)


def lagged(eng, count, prep, main):
    prep(0, 0)
    with eng.Fori(0, count // 2 - 1) as i:
        for h in range(2):
            prep(2 * i + h + 1, 1 - h)
            main(2 * i + h, h)
    prep(count - 1, 1)
    main(count - 2, 0)
    main(count - 1, 1)


class Chain:

    def __init__(self, eng, sem, first):
        self.eng, self.sem, self.value = eng, sem, first

    def then(self, ins):
        ins.then_inc(self.sem, 1)
        self.value = self.value + 1
        self.eng.wait_ge(self.sem, self.value)


def bc(ap, axis, shape):
    return ap.unsqueeze(axis).to_broadcast(shape)


def settle(eng, tick):
    eng.sem_inc(tick, 1)


def release(nc, sems):
    nc.clear_and_free_semaphores(sems)
    nc.all_engine_barrier()


class Mem:
    pass


def allocate(nc, ctx, ins, out):
    m = Mem()

    def sb(name, shape, dt):
        return ctx.enter_context(nc.sbuf_tensor(name, shape, dt))

    def dram(name, shape, dt):
        return nc.dram_tensor(name, shape, dt, kind="Internal").ap()

    m.ins, m.out = ins, out
    m.s_all = sb("s_all", [P, T * P], BF16)
    m.src_i = sb("src_i", [P, FRONT + T], I32)
    m.dst_i = sb("dst_i", [P, FRONT + T], I32)
    m.row_i = sb("row_i", [P, FRONT + T], I32)
    m.src2_i = sb("src2_i", [P, FRONT + T], I32)
    m.row2_i = sb("row2_i", [P, FRONT + T], I32)
    m.dst_t = sb("dst_t", [P, T], F32)
    m.ew_t = sb("ew_t", [P, T], F32)
    m.em4 = sb("em4", [P, T, 4], F32)
    m.em3 = sb("em3", [P, T, 3], F32)
    m.dst_f = sb("dst_f", [R, CH, P], F32)
    m.before = sb("before", [R, CH], F32)
    m.after = sb("after", [R, CH], F32)
    m.e_t = sb("e_t", [P, T], F32)
    m.ident = sb("ident", [P, P], F32)
    m.w_gru = sb("w_gru", [P, 4 * D], F32)
    m.b_gru = sb("b_gru", [P, 2, 4 * D], BF16)
    m.ones3 = sb("ones3", [P, P], BF16)
    m.w_msg1 = sb("w_msg1", [P, 2, D], F32)
    m.b_msg1 = sb("b_msg1", [P, D], F32)
    m.w_node = sb("w_node", [P, D], F32)
    m.w_msg2 = sb("w_msg2", [96, 3, D], F32)
    m.w_att = sb("w_att", [D, D], F32)
    m.wl = sb("wl", [P, D], F32)
    m.wr = sb("wr", [P, D], F32)
    m.bias3 = sb("bias3", [P, D], F32)
    m.eps = sb("eps", [P, 1], F32)
    m.x = dram("x_work", [NP_, D], F32)
    m.a0 = dram("a_first", [NP_, D], F32)
    m.fa = [dram(f"fa_{k}", [NP_, 2 * D], F32) for k in range(3)]
    m.h2 = dram("h2_signed", [NP_, D], F32)
    m.nt = dram("node_type_padded", [NP_], I32)
    m.attr = dram("edge_attr_padded", [EP, 32], F32)
    m.dst_rows = dram("dst_rows", [T + 2, P], F32)
    m.cx = dram("carry_rows", [5, EP], F32)
    m.h3 = dram("h3_by_edge", [P, T, D], F32)
    return m


def set_up(nc, m):
    ins = m.ins
    sems = []

    def keep(s):
        sems.append(s)
        return s

    with ExitStack() as ctx:
        def sb(name, shape, dt):
            return ctx.enter_context(nc.sbuf_tensor(name, shape, dt))

        def ps(name, shape):
            return ctx.enter_context(nc.psum_tensor(name, shape, F32))

        def sem(name):
            return keep(nc.alloc_semaphore(name))

        raw = sb("raw", [R, 5, CH, P], I32)
        flat = sb("flat", [R, 5, CH, P], F32)
        prev = sb("prev", [R, CH, P], F32)
        same = sb("same", [R, CH, P], F32)
        tab = sb("tab", [P, 6, T], F32)
        zero = sb("zero", [P, GD * D], F32)
        izero = sb("izero", [P, 16], I32)
        minus = sb("minus", [2, P], F32)
        wl_rz = sb("wl_rz", [P, P], F32)
        wl_h = sb("wl_h", [D, P], F32)
        wl_i = sb("wl_i", [D, P], F32)
        wl_1 = sb("wl_1", [D, 4, D], F32)
        brow = sb("brow", [3, 2, 4 * D], F32)
        bh = sb("bh", [3, 4, 4 * D], F32)
        bpart = sb("bpart", [3, 3, 4 * D], BF16)
        att = sb("att", [D, 2], F32)
        att_b = sb("att_b", [D, 2, P], F32)
        w_attT = sb("w_attT", [D, D], F32)
        iota4 = sb("iota4", [P, 4], F32)
        dbc = sb("dbc", [P, RING, U * P], F32)
        oh = sb("oh", [P, RING, U, 4], BF16)
        cnt = sb("cnt", [4, RING, U * P], F32)
        pt = [ps(f"su_pt{k}", [P, 512]) for k in range(2)]
        pw = ps("su_pw", [P, 512])
        pv = ps("su_pv", [P, 512])
        pc = [ps(f"su_pc{k}", [4, 1024]) for k in range(2)]

        s_fill = sem("su_fill")
        s_tick = sem("su_tick")
        s_edges = sem("su_edges")
        s_w = sem("su_weights")
        s_copy = sem("su_copies")
        s_minus = sem("su_minus")
        s_id = sem("su_ident")
        s_dve = sem("su_dve")
        s_flat = sem("su_flat")
        s_rows = sem("su_dst_rows")
        s_nxt = sem("su_next")
        s_same = sem("su_same")
        s_pt = sem("su_turned")
        s_tab = sem("su_tab")
        s_wt = sem("su_w_turned")
        s_wc = sem("su_w_copied")
        s_prev = sem("su_prev")
        s_zero = sem("su_zero")
        s_parts = sem("su_bias_parts")
        s_bias = sem("su_bias_rows")
        s_dbc = [sem(f"su_dbc{k}") for k in range(RING)]
        s_s = sem("su_s")
        s_pc = sem("su_counts")
        s_cnt = sem("su_counts_copied")
        s_cx = [sem(f"su_cx{k}") for k in range(RING)]
        names = ("dst", "src", "edge_type_4", "edge_type_3", "edge_weight")
        full = 3 * R
        rest = E // P - full
        tail = E - (full + rest) * P
        block = ctx.enter_context(nc.Block())

        @block.sync
        def _(sp):
            sp.wait_ge(s_fill, 1)
            for a, name in enumerate(names):
                src = ins[name]
                to = raw if a < 4 else flat
                sp.dma_start(to[:, a, 0:3, :], src[0:full * P].rearrange("(c r p) -> r c p", c=3, p=P)).then_inc(s_edges, 16)
                sp.dma_start(to[0:rest, a, 3, :], src[full * P:(full + rest) * P].rearrange("(r p) -> r p", p=P)).then_inc(s_edges, 16)
                sp.dma_start(to[rest:rest + 1, a, 3, 0:tail], src[(full + rest) * P:E].rearrange("(o p) -> o p", o=1)).then_inc(s_edges, 16)
            sp.dma_start(wl_rz[:, 0:D], ins["L1_gnn_w_hh"][0:P]).then_inc(s_w, 16)
            sp.dma_start(wl_rz[:, D:P], ins["L1_gnn_w_ih"][0:P]).then_inc(s_w, 16)
            sp.dma_start(wl_h[:, 0:D], ins["L1_gnn_w_hh"][P:P + D]).then_inc(s_w, 16)
            sp.dma_start(wl_i[:, D:P], ins["L1_gnn_w_ih"][P:P + D]).then_inc(s_w, 16)
            sp.dma_start(wl_1[:], ins["L1_gnn_W"].rearrange("k h d -> h k d")).then_inc(s_w, 16)
            sp.dma_start(m.b_msg1[1:5, :], ins["L1_gnn_b"]).then_inc(s_w, 16)
            sp.dma_start(brow[:, 0, 0:3 * D], ins["L1_gnn_b_hh"].rearrange("(o n) -> o n", o=1).to_broadcast([3, 3 * D])).then_inc(s_w, 16)
            sp.dma_start(brow[:, 1, 0:3 * D], ins["L1_gnn_b_ih"].rearrange("(o n) -> o n", o=1).to_broadcast([3, 3 * D])).then_inc(s_w, 16)
            sp.dma_start(m.w_node[:], ins["L2_gnn_W_node"].rearrange("t k n -> (t k) n")).then_inc(s_w, 16)
            sp.dma_start(m.w_msg2[:], ins["L2_gnn_W_msg"].rearrange("t k n -> k t n")).then_inc(s_w, 16)
            sp.dma_start(m.w_att[:], ins["L3_gnn_W"]).then_inc(s_w, 16)
            sp.dma_start(att[:, 0:1], ins["L3_gnn_attn_l"].rearrange("(d o) -> d o", o=1)).then_inc(s_w, 16)
            sp.dma_start(att[:, 1:2], ins["L3_gnn_attn_r"].rearrange("(d o) -> d o", o=1)).then_inc(s_w, 16)
            sp.dma_start(m.bias3[:], ins["L3_gnn_bias"].rearrange("(o n) -> o n", o=1).to_broadcast([P, D])).then_inc(s_w, 16)
            sp.dma_start(m.dst_rows[0:T + 2:T + 1], minus[:]).then_inc(s_minus, 16)
            sp.wait_ge(s_flat, 1)
            sp.dma_start(m.dst_rows[1:T + 1].rearrange("(c r) p -> r c p", r=R), flat[:, 0]).then_inc(s_rows, 16)
            idle = (NP_ - N) // GD
            sp.dma_start(m.x[N:NP_].rearrange("(p k) d -> p (k d)", k=GD), zero[0:idle, 0:GD * D]).then_inc(s_copy, 16)
            sp.dma_start(m.nt[N:NP_].rearrange("(p k) -> p k", k=GD), izero[0:idle, 0:GD]).then_inc(s_copy, 16)
            sp.dma_start(m.attr[E:EP].rearrange("(p k) d -> p (k d)", p=16), zero[0:16, 0:11 * 32]).then_inc(s_copy, 16)
            sp.dma_start(m.x[0:N].rearrange("(a b c) d -> a b (c d)", a=16, b=25), ins["x"].rearrange("(a b c) d -> a b (c d)", a=16, b=25)).then_inc(s_copy, 16)
            sp.dma_start(m.nt[0:N].rearrange("(a b) -> a b", a=16), ins["node_type_2"].rearrange("(a b) -> a b", a=16)).then_inc(s_copy, 16)
            sp.dma_start(m.attr[0:E].rearrange("(a b) d -> a (b d)", a=80), ins["edge_attr_32"].rearrange("(a b) d -> a (b d)", a=80)).then_inc(s_copy, 16)
            sp.wait_ge(s_rows, 16)
            sp.wait_ge(s_minus, 16)
            with nc.allow_non_contiguous_dma(reason="one dst of each tile"):
                sp.dma_start(m.after[:], m.dst_rows[2:T + 2, 0].rearrange("(c r) -> r c", r=R)).then_inc(s_nxt, 16)
                sp.dma_start(m.before[:], m.dst_rows[0:T, P - 1].rearrange("(c r) -> r c", r=R)).then_inc(s_nxt, 16)
            sp.wait_ge(s_parts, 1)
            for k in range(3):
                sp.dma_start(m.b_gru[k:k + 1, 0, :], bpart[k:k + 1, k, :]).then_inc(s_bias, 16)
                sp.dma_start(m.b_gru[k:k + 1, 1, :], bpart[k:k + 1, k, :]).then_inc(s_bias, 16)
            sp.wait_ge(s_same, 1)
            sp.dma_start(m.cx[0].rearrange("(c r p) -> r c p", r=R, p=P), same[:]).then_inc(s_copy, 16)

            def load(n, h):
                sp.wait_ge(s_s, n + 1)
                settle(sp, s_tick)
                rows = m.dst_rows[bass.ds(tile_base(n) + 1, U)].rearrange("t p -> (t p)")
                sp.dma_start(dbc[:, h, :], bc(rows, 0, [P, U * P])).then_inc(s_dbc[h], 16)

            def store(n, h):
                sp.wait_ge(s_cnt, n + 1 + RING)
                settle(sp, s_tick)
                sp.dma_start(m.cx[1:5, bass.ds(tile_base(n) * P, U * P)], cnt[:, h, :]).then_inc(s_cx[h], 16)

            lagged(sp, NG, load, store)
            sp.wait_ge(s_edges, 16 * 15)
            sp.wait_ge(s_w, 16 * 14)
            sp.wait_ge(s_copy, 16 * 7)
            sp.wait_ge(s_nxt, 32)
            sp.wait_ge(s_bias, 16 * 6)
            for h in range(RING):
                sp.wait_ge(s_cx[h], 16 * (NG // 2))

        @block.gpsimd
        def _(pool):
            nc.gpsimd.memset(m.ident[:], 0.0).then_inc(s_id, 1)
            nc.gpsimd.iota(iota4[:], [[1, 4]], base=0, channel_multiplier=0, allow_small_or_imprecise_dtypes=True).then_inc(s_id, 1)
            pool.wait_ge(s_id, 2)
            nc.gpsimd.affine_select(out=m.ident[:], in_=m.ident[:], compare_op=ALU.not_equal, fill=1.0, base=0,
                                    pattern=[[-1, P]], channel_multiplier=1).then_inc(s_id, 1)

        @block.tensor
        def _(pe):
            pe.wait_ge(s_id, 3)
            pe.wait_ge(s_flat, 1)
            for a in range(5):
                if a >= 2:
                    pe.wait_ge(s_tab, a - 1)
                for c in range(CH):
                    mm = pe.transpose(pt[a % 2][:, c * R:(c + 1) * R], flat[:, a, c, :], m.ident[0:R, 0:R])
                mm.then_inc(s_pt, 1)
            pe.wait_ge(s_tab, 4)
            pe.wait_ge(s_prev, 1)
            for c in range(CH):
                mm = pe.transpose(pt[1][:, c * R:(c + 1) * R], prev[:, c, :], m.ident[0:R, 0:R])
            mm.then_inc(s_pt, 1)
            pe.wait_ge(s_w, 16 * 14)
            pe.transpose(pw[:, 0:P], wl_rz[:], m.ident[:])
            pe.transpose(pw[:, P:P + D], wl_h[:], m.ident[0:D, 0:D])
            pe.transpose(pw[:, P + D:P + 2 * D], wl_i[:], m.ident[0:D, 0:D])
            for c in range(2):
                pe.transpose(pw[:, 4 * D + c * D:4 * D + (c + 1) * D], wl_1[:, 2 * c:2 * c + 2, :].rearrange("h k d -> h (k d)"), m.ident[0:D, 0:D])
            pe.transpose(pv[0:D, 0:D], m.w_att[:], m.ident[0:D, 0:D]).then_inc(s_wt, 1)
            pe.wait_ge(s_wc, 2)
            for a in range(2):
                mm = pe.matmul(pv[:, P + a * D:P + (a + 1) * D], lhsT=att_b[:, a, :], rhs=w_attT[:], start=True, stop=True)
            mm.then_inc(s_wt, 1)

            def counts(n, h):
                pe.wait_ge(s_s, n + 1 + RING)
                pe.wait_ge(s_cnt, n + 1)
                for k in range(U):
                    mm = pe.matmul(pc[h][:, k * P:(k + 1) * P], lhsT=oh[:, h, k, :],
                                   rhs=m.s_all[:, bass.ds((tile_base(n) + k) * P, P)], start=True, stop=True)
                mm.then_inc(s_pc, 1)

            with pe.Fori(0, NG // 2) as i:
                for h in range(2):
                    counts(2 * i + h, h)

        @block.scalar
        def _(act):
            act.sem_inc(s_cnt, RING)
            act.wait_ge(s_fill, 1)
            a0 = m.a0.rearrange("(g p k) d -> g p (k d)", p=P, k=GD)
            with act.Fori(0, ND) as g:
                act.dma_start(a0[bass.ds(g, 1)].rearrange("o p f -> (o p) f"), zero[:]).then_inc(s_zero, 16)
            with act.Fori(0, NG // 2) as i:
                for h in range(2):
                    act.wait_ge(s_pc, 2 * i + h + 1)
                    act.wait_ge(s_cx[h], 16 * i)
                    nc.scalar.copy(cnt[:, h, :], pc[h][:, 0:U * P]).then_inc(s_cnt, 1)
            act.wait_ge(s_zero, 16 * ND)

        @block.vector
        def _(dve):
            nc.vector.memset(raw[:, 0:2], int(FAR))
            nc.vector.memset(raw[:, 2:4], 0)
            nc.vector.memset(flat[:], 0.0)
            nc.vector.memset(zero[:], 0.0)
            nc.vector.memset(izero[:], 0)
            nc.vector.memset(minus[:], -1.0)
            nc.vector.memset(wl_h[:], 0.0)
            nc.vector.memset(wl_i[:], 0.0)
            nc.vector.memset(brow[:], 0.0)
            nc.vector.memset(m.b_msg1[:], 0.0)
            nc.vector.memset(m.b_gru[:], 0.0)
            nc.vector.memset(m.ones3[:], 0.0).then_inc(s_dve, 1)
            ch = Chain(dve, s_dve, 1)
            dve.wait_ge(s_dve, 1)
            ch.then(nc.vector.memset(m.ones3[0:3, :], 1.0))
            nc.vector.memset(m.eps[:], EPS)
            for t in (m.src_i, m.dst_i, m.row_i, m.src2_i, m.row2_i):
                nc.vector.memset(t[:, 0:FRONT], int(FAR))
            nc.vector.memset(prev[:], 0.0).then_inc(s_fill, 1)
            dve.wait_ge(s_edges, 16 * 15)
            ch.then(nc.vector.tensor_copy(flat[:, 0:4], raw[:, 0:4]))
            nc.vector.tensor_copy(m.dst_f[:], flat[:, 0])
            ch.then(nc.vector.tensor_copy(prev[:, :, 1:P], flat[:, 0, :, 0:P - 1]))
            dve.sem_inc(s_flat, 1)
            for a in range(5):
                dve.wait_ge(s_pt, a + 1)
                nc.vector.tensor_copy(tab[:, a, :], pt[a % 2][:, 0:T]).then_inc(s_tab, 1)
            dve.wait_ge(s_nxt, 32)
            nc.vector.tensor_tensor(same[:], flat[:, 0], bc(m.after[:], 2, [R, CH, P]), ALU.is_equal).then_inc(s_same, 1)
            nc.vector.tensor_copy(prev[:, :, 0], m.before[:]).then_inc(s_prev, 1)
            dve.wait_ge(s_pt, 6)
            nc.vector.tensor_copy(tab[:, 5, :], pt[1][:, 0:T]).then_inc(s_tab, 1)
            dve.wait_ge(s_tab, 6)
            dst, src = tab[:, 0, :], tab[:, 1, :]
            nc.vector.tensor_copy(m.dst_t[:], dst)
            nc.vector.tensor_copy(m.ew_t[:], tab[:, 4, :])
            nc.vector.tensor_copy(m.src_i[:, FRONT:], src)
            nc.vector.tensor_copy(m.dst_i[:, FRONT:], dst)
            nc.vector.tensor_scalar(m.src2_i[:, FRONT:], src, 2.0, None, ALU.mult)
            ch.then(nc.vector.tensor_tensor(tab[:, 5, :], tab[:, 5, :], dst, ALU.is_equal))
            ch.then(nc.vector.scalar_tensor_tensor(out=tab[:, 5, :], in0=tab[:, 5, :], scalar=FAR, in1=dst, op0=ALU.mult, op1=ALU.add))
            nc.vector.tensor_copy(m.row_i[:, FRONT:], tab[:, 5, :])
            nc.vector.tensor_scalar(m.row2_i[:, FRONT:], tab[:, 5, :], 2.0, 1.0, ALU.mult, ALU.add)
            for k in range(4):
                nc.vector.tensor_scalar(m.em4[:, :, k], tab[:, 2, :], float(k), None, ALU.is_equal)
            for k in range(3):
                ins_ = nc.vector.tensor_scalar(m.em3[:, :, k], tab[:, 3, :], float(k), None, ALU.is_equal)
            ch.then(ins_)
            dve.wait_ge(s_wt, 1)
            ch.then(nc.vector.tensor_copy(m.w_msg1[:].rearrange("p c d -> p (c d)"), pw[:, 4 * D:6 * D]))
            nc.vector.tensor_copy(m.w_gru[:, 0:4 * D], pw[:, 0:4 * D])
            nc.vector.tensor_copy(w_attT[:], pv[0:D, 0:D]).then_inc(s_wc, 1)
            nc.vector.tensor_copy(att_b[:], bc(att[:], 2, [D, 2, P])).then_inc(s_wc, 1)
            dve.wait_ge(s_wt, 2)
            nc.vector.tensor_copy(m.wl[:], pv[:, P:P + D])
            nc.vector.tensor_copy(m.wr[:], pv[:, P + D:P + 2 * D])
            ch.then(nc.vector.tensor_tensor(bh[:, 0, 0:2 * D], brow[:, 0, 0:2 * D], brow[:, 1, 0:2 * D], ALU.add))
            ch.then(nc.vector.tensor_copy(bh[:, 0, 2 * D:3 * D], brow[:, 0, 2 * D:3 * D]))
            ch.then(nc.vector.tensor_copy(bh[:, 0, 3 * D:4 * D], brow[:, 1, 2 * D:3 * D]))
            ch.then(nc.vector.tensor_copy(bpart[:, 0, :], bh[:, 0, :]))
            ch.then(nc.vector.tensor_tensor(bh[:, 1, :], bh[:, 0, :], bpart[:, 0, :], ALU.subtract))
            ch.then(nc.vector.tensor_copy(bpart[:, 1, :], bh[:, 1, :]))
            ch.then(nc.vector.tensor_tensor(bh[:, 2, :], bh[:, 1, :], bpart[:, 1, :], ALU.subtract))
            nc.vector.tensor_copy(bpart[:, 2, :], bh[:, 2, :]).then_inc(s_parts, 1)
            dve.sem_inc(s_s, RING)
            with dve.Fori(0, NG // 2) as i:
                for h in range(2):
                    n = 2 * i + h
                    dve.wait_ge(s_dbc[h], 16 * i + 16)
                    dve.wait_ge(s_cnt, n + 1)
                    nc.vector.tensor_copy(oh[:, h], m.em4[:, bass.ds(tile_base(n), U), :])
                    nc.vector.tensor_tensor(m.s_all[:, bass.ds(tile_base(n) * P, U * P)].rearrange("p (t s) -> p t s", t=U),
                                            dbc[:, h, :].rearrange("p (t s) -> p t s", t=U),
                                            bc(m.dst_t[:, bass.ds(tile_base(n), U)], 2, [P, U, P]), ALU.is_equal).then_inc(s_s, 1)
    release(nc, sems)


def edge_round(nc, m, kind, table=None, target=None):
    gather = kind != "attend"
    norm = kind in ("sum", "first")
    graph = kind in ("first", "step")
    wide = graph or kind == "typed"
    blocks = 2 if graph else 3
    rows = P if graph else 96
    W = D + 1 if kind == "attend" else D
    uid = nc.next_id()
    DONE = 2 * U
    sems = []

    def keep(s):
        sems.append(s)
        return s

    with ExitStack() as ctx:
        def sb(name, shape, dt=F32):
            return ctx.enter_context(nc.sbuf_tensor(f"{kind}{uid}_{name}", shape, dt))

        def ps(name, shape):
            return ctx.enter_context(nc.psum_tensor(f"{kind}{uid}_{name}", shape, F32))

        def sem(name):
            return keep(nc.alloc_semaphore(f"{kind}{uid}_{name}"))

        s_f32 = sb("s_f32", [P, RING, U * P])
        cx = sb("cx", [P, RING, U * P])
        car = sb("car", [P, RING, W])
        o = sb("o", [P, RING, U, D])
        row_s = sb("row_s", [P, RING, U], I32)
        p_out = [ps(f"p_out{k}", [P, 512]) for k in range(RING)]
        if gather:
            idx = sb("idx", [P, RING, U], I32)
            g = sb("g", [P, RING, U, D])
        if norm:
            cen = sb("cen", [P, U, D])
            sq = sb("sq", [P, U, D])
            stat = sb("stat", [P, 4, U])
            msg = sb("msg", [P, RING, U, D])
        if wide:
            p_sum = [ps(f"p_sum{k}", [P, 512]) for k in range(RING)]
            agg = sb("agg", [P, RING, blocks * P])
        if graph:
            fm = sb("fm", [P, RING, U, 4, D])
        if kind == "typed":
            pos = sb("pos", [P, RING, U, 2, D])
            posT = sb("posT", [P, U * P])
            attr = sb("attr", [P, RING, U, 32])
            xm = sb("xm", [P, RING, U, 3, 96])
            p_turn = [ps(f"p_turn{k}", [P, 512]) for k in range(2)]
            p_x = ps("p_x", [P, 512])
        if kind == "attend":
            h3 = sb("h3", [P, RING, U, D])
            msg = sb("msg", [P, RING, U, W])
            both = sb("both", [P, RING, U, W])
            den = sb("den", [P, 2, U])
            val = sb("val", [P, U, D])
            valT = sb("valT", [D, U * P])
            p_turn = [ps(f"p_turn{k}", [D, 512]) for k in range(2)]
            p_w = ps("p_w", [P, 512])

        s_init = sem("init")
        s_tick = sem("tick")
        s_idx = sem("indices_staged")
        s_g = [sem(f"gathered{k}") for k in range(RING)]
        s_cx = [sem(f"carry_rows{k}") for k in range(RING)]
        s_in = [sem(f"loaded{k}") for k in range(RING)]
        s_s = sem("s_ready")
        s_prep = sem("prep_chain")
        s_cen = sem("centered")
        s_sq = sem("squared")
        s_dev = sem("deviation")
        s_msg = sem("messages_ready")
        s_sum = sem("tiles_summed")
        s_part = sem("parts_summed")
        s_agg = sem("parts_copied")
        s_car = sem("carry_ready")
        s_o = sem("rows_ready")
        s_row = sem("row_indices")
        s_sc = [sem(f"scattered{k}") for k in range(RING)]
        s_t = sem("turned")
        s_tc = sem("turned_copied")
        s_x = sem("transformed")
        s_val = sem("values")
        s_w = sem("values_transformed")
        block = ctx.enter_context(nc.Block())
        src_i = m.src2_i if kind == "step" else m.src_i
        row_i = m.row2_i if kind == "step" else m.row_i
        bound = (2 * N if kind == "step" else N) - 1

        @block.sync
        def _(sp):
            sp.wait_ge(s_init, 1)

            def load(n, h, i):
                sp.wait_ge(s_sum, U * (n + 1))
                settle(sp, s_tick)
                rows_ = 5 if graph else 1
                sp.dma_start(cx[0:rows_, h, :], m.cx[0:rows_, bass.ds(tile_base(n) * P, U * P)]).then_inc(s_cx[h], 16)
                if kind == "typed":
                    view = m.attr.rearrange("(t p) f -> p t f", p=P)
                    sp.dma_start(attr[:, h], view[:, bass.ds(tile_base(n), U), :]).then_inc(s_in[h], 16)
                if kind == "attend":
                    sp.dma_start(h3[:, h], m.h3[:, bass.ds(tile_base(n), U), :]).then_inc(s_in[h], 16)

            with sp.Fori(0, NG // 2) as i:
                for h in range(2):
                    load(2 * i + h, h, i)

        @block.gpsimd
        def _(pool):
            limit = pool.to_reg(bound)

            def fetch(n, h):
                pool.wait_ge(s_idx, n + 1)
                settle(pool, s_tick)
                for k in range(U):
                    nc.gpsimd.indirect_dma_start(
                        out=g[:, h, k, :], out_offset=None, in_=table,
                        in_offset=bass.IndirectOffsetOnAxis(ap=idx[:, h, k:k + 1], axis=0),
                        bounds_check=limit, oob_is_err=False).then_inc(s_g[h], 16)

            def scatter(n, h):
                pool.wait_ge(s_row, n + 1)
                if kind == "attend":
                    pool.wait_ge(s_o, n + 1)
                else:
                    pool.wait_ge(s_o, U * (n + 1) + RING)
                settle(pool, s_tick)
                for k in range(U):
                    nc.gpsimd.indirect_dma_start(
                        out=target, out_offset=bass.IndirectOffsetOnAxis(ap=row_s[:, h, k:k + 1], axis=0),
                        in_=o[:, h, k, :], in_offset=None, bounds_check=limit, oob_is_err=False,
                        **({} if graph else {"compute_op": ALU.add})).then_inc(s_sc[h], 16)

            if gather:
                fetch(0, 0)
                fetch(1, 1)
                with pool.Fori(0, NG // 2 - 1) as i:
                    for h in range(2):
                        fetch(2 * i + h + 2, h)
                        scatter(2 * i + h, h)
                scatter(NG - 2, 0)
                scatter(NG - 1, 1)
            else:
                with pool.Fori(0, NG // 2) as i:
                    for h in range(2):
                        scatter(2 * i + h, h)
            for h in range(RING):
                pool.wait_ge(s_sc[h], 16 * U * (NG // 2))

        @block.tensor
        def _(pe):
            pe.sem_inc(s_sum, DONE)
            pe.wait_ge(s_init, 1)

            def prep(n, h):
                pe.wait_ge(s_prep, 2 * n + 2)
                for k in range(U):
                    mm = pe.transpose(p_turn[k // 4][:, k % 4 * P:(k % 4 + 1) * P],
                                      pos[:, h, k].rearrange("p a d -> p (a d)"), m.ident[:])
                mm.then_inc(s_t, 1)
                pe.wait_ge(s_tc, n + 1)
                pe.wait_ge(s_msg, n)
                for k in range(U):
                    mm = pe.matmul(p_x[:, k * D:(k + 1) * D], lhsT=posT[:, k * P:(k + 1) * P], rhs=m.w_node[:], start=True, stop=True)
                mm.then_inc(s_x, 1)

            def parts(q, h, k, slot):
                pe.wait_ge(s_agg, q + 1)
                for c in range(blocks):
                    lhs = fm[:, h, k, 2 * c:2 * c + 2, :].rearrange("p a d -> p (a d)") if graph else xm[:, h, k, c, :]
                    mm = pe.matmul(p_sum[slot][0:rows, c * P:(c + 1) * P], lhsT=lhs, rhs=s_f32[:, h, k * P:(k + 1) * P], start=True, stop=True)
                mm.then_inc(s_part, 1)

            def total(q, h, k, slot):
                if kind != "attend":
                    pe.wait_ge(s_o, q + 1)
                to = p_out[slot][:, 0:W]
                if wide:
                    pe.wait_ge(s_agg, q + 1 + RING)
                    for c in range(blocks):
                        w = m.w_msg1[:, c, :] if graph else m.w_msg2[:, c, :]
                        pe.matmul(to, lhsT=agg[0:rows, slot, c * P:(c + 1) * P], rhs=w, start=(c == 0), stop=False)
                else:
                    pe.matmul(to, lhsT=s_f32[:, h, k * P:(k + 1) * P], rhs=msg[:, h, k, :], start=True, stop=False)
                pe.wait_ge(s_car, q + 1)
                pe.matmul(to, lhsT=cx[:, h, k * P:(k + 1) * P], rhs=car[:, slot, :], start=False, stop=True).then_inc(s_sum, 1)

            def main(n, h):
                pe.wait_ge(s_msg, n + 1)
                pe.wait_ge(s_s, n + 1)
                pe.wait_ge(s_cx[h], 8 * (n - h) + 16)
                for j in range(U):
                    if wide:
                        parts(U * n + j, h, U - 1 - j, (U * h + j) % RING)
                        if j >= 1:
                            total(U * n + j - 1, h, U - j, (U * h + j - 1) % RING)
                    else:
                        total(U * n + j, h, U - 1 - j, (U * h + j) % RING)
                if wide:
                    total(U * n + U - 1, h, 0, (U * h + U - 1) % RING)
                if kind == "attend":
                    pe.wait_ge(s_val, n + 1)
                    settle(pe, s_tick)
                    for k in range(U):
                        mm = pe.transpose(p_turn[k // 4][:, k % 4 * P:(k % 4 + 1) * P], val[:, k, :], m.ident[:])
                    mm.then_inc(s_t, 1)
                    pe.wait_ge(s_tc, n + 1)
                    pe.wait_ge(s_o, n)
                    for k in range(U):
                        mm = pe.matmul(p_w[:, k * D:(k + 1) * D], lhsT=valT[:, k * P:(k + 1) * P], rhs=m.w_att[:], start=True, stop=True)
                    mm.then_inc(s_w, 1)

            if kind == "typed":
                lagged(pe, NG, prep, main)
            else:
                with pe.Fori(0, NG // 2) as i:
                    for h in range(2):
                        main(2 * i + h, h)

        @block.scalar
        def _(act):
            if wide:
                act.sem_inc(s_agg, RING)

            def prep(n, h):
                if norm:
                    act.wait_ge(s_cen, n + 1)
                    nc.scalar.activation(sq[:], cen[:], ACT.Square).then_inc(s_sq, 1)
                act.wait_ge(s_sum, U * (n + 1))
                nc.scalar.copy(s_f32[:, h, :], m.s_all[:, bass.ds(tile_base(n) * P, U * P)]).then_inc(s_s, 1)
                if norm:
                    act.wait_ge(s_dev, 2 * n + 1)
                    nc.scalar.activation(stat[:, 2, :], stat[:, 1, :], ACT.Sqrt, bias=m.eps[:, 0:1], scale=1.0 / D).then_inc(s_dev, 1)
                if kind == "typed":
                    act.wait_ge(s_t, n + 1)
                    if not (isinstance(n, int) and n == 0):
                        act.wait_ge(s_x, n)
                    nc.scalar.copy(posT[:, 0:4 * P], p_turn[0][:])
                    nc.scalar.copy(posT[:, 4 * P:], p_turn[1][:, 0:3 * P]).then_inc(s_tc, 1)

            def main(n, h):
                if wide:
                    for j in range(U):
                        q, slot = U * n + j, (U * h + j) % RING
                        act.wait_ge(s_part, q + 1)
                        act.wait_ge(s_sum, q + 1 + DONE - RING)
                        nc.scalar.copy(agg[0:rows, slot, :], p_sum[slot][0:rows, 0:blocks * P]).then_inc(s_agg, 1)
                if kind == "attend":
                    act.wait_ge(s_t, n + 1)
                    nc.scalar.copy(valT[:, 0:4 * P], p_turn[0][:])
                    nc.scalar.copy(valT[:, 4 * P:], p_turn[1][:, 0:3 * P]).then_inc(s_tc, 1)
                    act.wait_ge(s_w, n + 1)
                    act.wait_ge(s_sc[h], 8 * U * (n - h))
                    nc.scalar.copy(o[:, h].rearrange("p k d -> p (k d)"), p_w[:, 0:U * D]).then_inc(s_o, 1)

            lagged(act, NG, prep, main)

        @block.vector
        def _(dve):
            nc.vector.memset(cx[:], 0.0)
            nc.vector.memset(car[:], 0.0).then_inc(s_car, 1)
            dve.wait_ge(s_car, 1)
            if gather:
                nc.vector.memset(g[:], 0.0)
            if graph:
                for slot in range(RING):
                    nc.vector.tensor_copy(car[:, slot, :], m.b_msg1[:])
            nc.vector.memset(o[:], 0.0).then_inc(s_init, 1)
            dve.wait_ge(s_init, 1)
            if kind != "attend":
                dve.sem_inc(s_o, RING)
            if gather:
                for n in range(RING):
                    nc.vector.tensor_copy(idx[:, n, :], src_i[:, FRONT + tile_base(n):FRONT + tile_base(n) + U]).then_inc(s_idx, 1)

            def refill(n, h):
                nc.vector.tensor_copy(idx[:, h, :], src_i[:, bass.ds(FRONT + tile_base(n + 2), U)]).then_inc(s_idx, 1)

            def prep(n, h):
                i16 = 8 * (n - h) + 16
                if gather:
                    dve.wait_ge(s_g[h], U * i16)
                if norm:
                    ch = Chain(dve, s_prep, 3 * n)
                    ch.then(nc.vector.tensor_reduce(stat[:, 0, :], g[:, h], AX.X, ALU.add))
                    nc.vector.scalar_tensor_tensor(out=cen[:], in0=bc(stat[:, 0, :], 2, [P, U, D]), scalar=-1.0 / D,
                                                   in1=g[:, h], op0=ALU.mult, op1=ALU.add).then_inc(s_cen, 1)
                    dve.wait_ge(s_sq, n + 1)
                    refill(n, h)
                    nc.vector.tensor_reduce(stat[:, 1, :], sq[:], AX.X, ALU.add).then_inc(s_dev, 1)
                    dve.wait_ge(s_dev, 2 * n + 2)
                    ch.then(nc.vector.reciprocal(stat[:, 3, :], stat[:, 2, :]))
                    if kind == "sum":
                        ch.then(nc.vector.tensor_tensor(stat[:, 3, :], stat[:, 3, :], m.ew_t[:, bass.ds(tile_base(n), U)], ALU.mult))
                    dve.wait_ge(s_sum, U * (n + 1))
                    ins_ = nc.vector.scalar_tensor_tensor(out=msg[:, h], in0=cen[:], scalar=0.0, in1=bc(stat[:, 3, :], 2, [P, U, D]),
                                                          op0=ALU.max, op1=ALU.mult)
                    if kind == "sum":
                        ins_.then_inc(s_msg, 1)
                    else:
                        ch.then(ins_)
                if graph:
                    dve.wait_ge(s_sum, U * (n + 1))
                    settle(dve, s_tick)
                    rows_in = msg[:, h] if norm else g[:, h]
                    mask = m.em4[:, bass.ds(tile_base(n), U), :]
                    nc.vector.tensor_tensor(fm[:, h], bc(rows_in, 2, [P, U, 4, D]), bc(mask, 3, [P, U, 4, D]), ALU.mult).then_inc(s_msg, 1)
                    if not norm:
                        dve.wait_ge(s_msg, n + 1)
                        refill(n, h)
                if kind == "typed":
                    ch = Chain(dve, s_prep, 2 * n)
                    ch.then(nc.vector.tensor_scalar(pos[:, h, :, 0, :], g[:, h], 0.0, None, ALU.max))
                    ch.then(nc.vector.tensor_scalar(pos[:, h, :, 1, :], g[:, h], -1.0, 0.0, ALU.mult, ALU.max))
                    refill(n, h)
                    dve.wait_ge(s_in[h], i16)
                    dve.wait_ge(s_sum, U * (n + 1))
                    settle(dve, s_tick)
                    mask = m.em3[:, bass.ds(tile_base(n), U), :]
                    nc.vector.tensor_tensor(xm[:, h, :, :, D:96], bc(attr[:, h], 2, [P, U, 3, 32]), bc(mask, 3, [P, U, 3, 32]), ALU.mult)
                    dve.wait_ge(s_x, n + 1)
                    nc.vector.tensor_tensor(xm[:, h, :, :, 0:D], bc(p_x[:, 0:U * D].rearrange("p (k d) -> p k d", k=U), 2, [P, U, 3, D]),
                                            bc(mask, 3, [P, U, 3, D]), ALU.mult).then_inc(s_msg, 1)
                if kind == "attend":
                    dve.wait_ge(s_in[h], i16)
                    dve.wait_ge(s_sum, U * (n + 1))
                    settle(dve, s_tick)
                    e = m.e_t[:, bass.ds(tile_base(n), U)]
                    nc.vector.tensor_copy(msg[:, h, :, D:W].rearrange("p k o -> p (k o)"), e)
                    nc.vector.tensor_tensor(msg[:, h, :, 0:D], h3[:, h], bc(e, 2, [P, U, D]), ALU.mult).then_inc(s_msg, 1)

            def main(n, h):
                dve.wait_ge(s_sc[h], 8 * U * (n - h))
                nc.vector.tensor_copy(row_s[:, h, :], row_i[:, bass.ds(FRONT + tile_base(n), U)]).then_inc(s_row, 1)
                for j in range(U):
                    q, k, slot = U * n + j, U - 1 - j, (U * h + j) % RING
                    dve.wait_ge(s_sum, q + 1 + DONE)
                    if kind == "attend":
                        nc.vector.tensor_copy(both[:, h, k, :], p_out[slot][:, 0:W])
                        nc.vector.tensor_copy(car[0:1, 1 - slot, :], p_out[slot][0:1, 0:W]).then_inc(s_car, 1)
                    else:
                        nc.vector.tensor_copy(car[0:1, 1 - slot, :], p_out[slot][0:1, 0:W]).then_inc(s_car, 1)
                        nc.vector.tensor_copy(o[:, h, k, :], p_out[slot][:, 0:W]).then_inc(s_o, 1)
                if kind == "attend":
                    ch = Chain(dve, s_prep, 2 * n)
                    dve.wait_ge(s_car, U * (n + 1) + 1)
                    total = both[:, h, :, D:W].rearrange("p k o -> p (k o)")
                    ch.then(nc.vector.scalar_tensor_tensor(out=den[:, 0, :], in0=total, scalar=0.0, in1=total, op0=ALU.is_equal, op1=ALU.add))
                    ch.then(nc.vector.reciprocal(den[:, 1, :], den[:, 0, :]))
                    dve.wait_ge(s_t, n)
                    nc.vector.tensor_tensor(val[:], both[:, h, :, 0:D], bc(den[:, 1, :], 2, [P, U, D]), ALU.mult).then_inc(s_val, 1)

            lagged(dve, NG, prep, main)
    release(nc, sems)


def dense_step(nc, m, step, table, target):
    first, last = step == 0, step == 3
    Q = 4
    sems = []

    def keep(s):
        sems.append(s)
        return s

    with ExitStack() as ctx:
        def sb(name, shape, dt=F32):
            return ctx.enter_context(nc.sbuf_tensor(f"d{step}_{name}", shape, dt))

        def sem(name):
            return keep(nc.alloc_semaphore(f"dense{step}_{name}"))

        fa = sb("fa", [P, RING, GD, 2 * D])
        faT = sb("faT", [P, RING, Q * P])
        fo = sb("fo", [P, RING, GD, 2 * D])
        rz = sb("rz", [P, RING, Q, 2 * D])
        tmp = sb("tmp", [P, RING, Q, D])
        pre = sb("pre", [P, RING, Q, D])
        cand = sb("cand", [P, RING, Q, D])
        p_t = [ctx.enter_context(nc.psum_tensor(f"d{step}_pt{k}", [P, 512], F32)) for k in range(RING)]
        p_g = [ctx.enter_context(nc.psum_tensor(f"d{step}_pg{k}", [P, Q, 4 * D], F32)) for k in range(RING)]
        if first or last:
            x = sb("x", [P, RING, GD, D])
            x_new = sb("x_new", [P, RING, GD, D]) if last else None
            cen = sb("cen", [P, GD, D])
            sq = sb("sq", [P, GD, D])
            stat = sb("stat", [P, 4, GD])
            half = sb("half", [P, GD])
        if last:
            nt = sb("nt", [P, RING, GD], I32)
            sign = sb("sign", [P, GD])
            h2 = sb("h2", [P, RING, GD, D])
        s_in = [sem(f"loaded{k}") for k in range(RING)]
        s_out = [sem(f"stored{k}") for k in range(RING)]
        s_init = sem("init")
        s_tick = sem("tick")
        s_free = sem("slot_read")
        s_f = sem("f_ready")
        s_t = sem("turned")
        s_tc = sem("turned_copied")
        s_g = sem("gates")
        s_rz = sem("rz_ready")
        s_pre = sem("pre_ready")
        s_cand = sem("cand_ready")
        s_fo = sem("fo_ready")
        s_a = sem("a_copied")
        s_up = sem("update_chain")
        s_ln = sem("norm_chain")
        s_dev = sem("deviation")
        s_res = sem("results")
        block = ctx.enter_context(nc.Block())
        parts = 2 if first else (3 if last else 1)
        NV = 2 * ND

        def group(ap, n):
            v = ap.rearrange("(g p k) d -> g p (k d)", p=P, k=GD)
            return v[bass.ds(n, 1)].rearrange("o p f -> (o p) f")

        @block.sync
        def _(sp):
            def load(n, h):
                sp.wait_ge(s_free, n + 1)
                settle(sp, s_tick)
                if first:
                    sp.dma_start(fa[:, h, :, D:2 * D], group(m.a0, n).rearrange("p (k d) -> p k d", k=GD)).then_inc(s_in[h], 16)
                else:
                    sp.dma_start(fa[:, h].rearrange("p k d -> p (k d)"), group(table, n)).then_inc(s_in[h], 16)
                if first or last:
                    sp.dma_start(x[:, h].rearrange("p k d -> p (k d)"), group(m.x, n)).then_inc(s_in[h], 16)
                if last:
                    v = m.nt.rearrange("(g p k) -> g p k", p=P, k=GD)
                    sp.dma_start(nt[:, h], v[bass.ds(n, 1)].rearrange("o p k -> (o p) k")).then_inc(s_in[h], 16)

            def store(n, h):
                if last:
                    sp.wait_ge(s_res, n + 1)
                    settle(sp, s_tick)
                    sp.dma_start(group(m.x, n), x_new[:, h].rearrange("p k d -> p (k d)")).then_inc(s_out[h], 16)
                    sp.dma_start(group(m.h2, n), h2[:, h].rearrange("p k d -> p (k d)")).then_inc(s_out[h], 16)
                else:
                    sp.wait_ge(s_fo, 2 * n + 2 + RING)
                    settle(sp, s_tick)
                    sp.wait_ge(s_a, n + 1)
                    settle(sp, s_tick)
                    sp.dma_start(group(target, n), fo[:, h].rearrange("p k d -> p (k d)")).then_inc(s_out[h], 16)

            load(0, 0)
            load(1, 1)
            with sp.Fori(0, ND // 2 - 1) as i:
                for h in range(2):
                    load(2 * i + h + 2, h)
                    store(2 * i + h, h)
            store(ND - 2, 0)
            store(ND - 1, 1)
            for h in range(RING):
                sp.wait_ge(s_out[h], (32 if last else 16) * (ND // 2))

        @block.gpsimd
        def _(pool):
            if first or last:
                nc.gpsimd.memset(half[:], -0.5).then_inc(s_init, 1)
                pool.wait_ge(s_init, 1)

            def power(n):
                pool.wait_ge(s_dev, 2 * n + 1)
                nc.gpsimd.tensor_tensor(stat[:, 2, :], stat[:, 1, :], half[:], ALU.pow).then_inc(s_dev, 1)

            def work(n, h):
                if first:
                    power(n)
                if last:
                    power(n)
                else:
                    pool.wait_ge(s_in[h], 8 * parts * (n - h) + 16 * parts)
                    pool.wait_ge(s_out[h], 8 * (n - h))
                    settle(pool, s_tick)
                    nc.gpsimd.tensor_copy(fo[:, h, :, D:2 * D], fa[:, h, :, D:2 * D]).then_inc(s_a, 1)

            with pool.Fori(0, ND // 2) as i:
                for h in range(2):
                    work(2 * i + h, h)

        @block.tensor
        def _(pe):
            def turn(v, h, u):
                pe.wait_ge(s_tc, v + 1)
                for k in range(Q):
                    mm = pe.transpose(p_t[u][:, k * P:(k + 1) * P], fa[:, h, u * Q + k, :], m.ident[:])
                mm.then_inc(s_t, 1)

            def gates(v, u):
                pe.wait_ge(s_pre, v + 1)
                for b in range(2):
                    pe.matmul(p_g[u][:, 2 * b:2 * b + 2, :].rearrange("p k d -> p (k d)"), lhsT=m.ones3[:],
                              rhs=m.b_gru[:].rearrange("p a d -> p (a d)"), start=True, stop=False, skip_group_check=True)
                pe.wait_ge(s_tc, v + 1 + RING)
                for k in range(Q):
                    mm = pe.matmul(p_g[u][:, k, :], lhsT=faT[:, u, k * P:(k + 1) * P], rhs=m.w_gru[:], start=False,
                                   stop=True, skip_group_check=True)
                mm.then_inc(s_g, 1)

            def ready(n, h):
                if first:
                    pe.wait_ge(s_f, n + 1)
                pe.wait_ge(s_in[h], 8 * parts * (n - h) + 16 * parts)

            ready(0, 0)
            turn(0, 0, 0)
            with pe.Fori(0, ND // 2 - 1) as i:
                for h in range(2):
                    v = 4 * i + 2 * h
                    turn(v + 1, h, 1)
                    gates(v, 0)
                    ready(2 * i + h + 1, 1 - h)
                    turn(v + 2, 1 - h, 0)
                    gates(v + 1, 1)
            turn(NV - 3, 0, 1)
            gates(NV - 4, 0)
            ready(ND - 1, 1)
            turn(NV - 2, 1, 0)
            gates(NV - 3, 1)
            turn(NV - 1, 1, 1)
            gates(NV - 2, 0)
            gates(NV - 1, 1)

        @block.scalar
        def _(act):
            act.sem_inc(s_tc, RING)

            def copy_turned(v, u):
                act.wait_ge(s_t, v + 1)
                act.wait_ge(s_g, v + 1)
                nc.scalar.copy(faT[:, u, :], p_t[u][:]).then_inc(s_tc, 1)

            def activate(v, u):
                act.wait_ge(s_g, v + 1 + RING)
                act.wait_ge(s_fo, v + 1)
                nc.scalar.activation(rz[:, u], p_g[u][:, :, 0:2 * D], ACT.Sigmoid).then_inc(s_rz, 1)
                act.wait_ge(s_pre, v + 1 + RING)
                nc.scalar.activation(cand[:, u], pre[:, u], ACT.Tanh).then_inc(s_cand, 1)

            copy_turned(0, 0)
            with act.Fori(0, NV // 2 - 1) as i:
                for u in range(2):
                    copy_turned(2 * i + u + 1, 1 - u)
                    activate(2 * i + u, u)
            copy_turned(NV - 1, 1)
            activate(NV - 2, 0)
            activate(NV - 1, 1)

        @block.vector
        def _(dve):
            dve.sem_inc(s_free, RING)
            dve.sem_inc(s_pre, RING)
            dve.sem_inc(s_g, RING)
            dve.sem_inc(s_fo, RING)
            CH_N = 5 if last else 4

            def norm(n, rows_in, rows_out, done, signs):
                ch = Chain(dve, s_ln, CH_N * n)
                ch.then(nc.vector.tensor_reduce(stat[:, 0, :], rows_in, AX.X, ALU.add))
                ch.then(nc.vector.scalar_tensor_tensor(out=cen[:], in0=bc(stat[:, 0, :], 2, [P, GD, D]), scalar=-1.0 / D,
                                                       in1=rows_in, op0=ALU.mult, op1=ALU.add))
                ch.then(nc.vector.tensor_tensor(sq[:], cen[:], cen[:], ALU.mult))
                ch.then(nc.vector.tensor_reduce(stat[:, 3, :], sq[:], AX.X, ALU.add))
                nc.vector.tensor_scalar(stat[:, 1, :], stat[:, 3, :], 1.0 / D, EPS, ALU.mult, ALU.add).then_inc(s_dev, 1)
                dve.wait_ge(s_dev, 2 * n + 2)
                if signs is not None:
                    ch.then(nc.vector.tensor_tensor(stat[:, 2, :], stat[:, 2, :], signs, ALU.mult))
                nc.vector.scalar_tensor_tensor(out=rows_out, in0=cen[:], scalar=0.0, in1=bc(stat[:, 2, :], 2, [P, GD, D]),
                                               op0=ALU.max, op1=ALU.mult).then_inc(done, 1)

            def prep(n, h):
                dve.wait_ge(s_in[h], 8 * parts * (n - h) + 16 * parts)
                norm(n, x[:, h], fa[:, h, :, 0:D], s_f, None)

            def half_one(v, h, u):
                dve.wait_ge(s_rz, v + 1)
                ch = Chain(dve, s_up, 3 * v)
                ch.then(nc.vector.tensor_tensor(tmp[:, u], rz[:, u, :, 0:D], p_g[u][:, :, 2 * D:3 * D], ALU.mult))
                nc.vector.tensor_tensor(pre[:, u], tmp[:, u], p_g[u][:, :, 3 * D:4 * D], ALU.add).then_inc(s_pre, 1)
                f = fa[:, h, u * Q:(u + 1) * Q, 0:D]
                dve.wait_ge(s_cand, v + 1)
                ch.then(nc.vector.tensor_tensor(tmp[:, u], f, cand[:, u], ALU.subtract))
                ch.then(nc.vector.tensor_tensor(tmp[:, u], tmp[:, u], rz[:, u, :, D:2 * D], ALU.mult))
                nc.vector.tensor_tensor(fo[:, h, u * Q:(u + 1) * Q, 0:D], tmp[:, u], cand[:, u], ALU.add).then_inc(s_fo, 1)

            def main(n, h):
                if not last:
                    dve.wait_ge(s_out[h], 8 * (n - h))
                for u in range(2):
                    half_one(2 * n + u, h, u)
                dve.wait_ge(s_fo, 2 * n + 2 + RING)
                if last:
                    dve.wait_ge(s_in[h], 8 * parts * (n - h) + 16 * parts)
                    dve.wait_ge(s_out[h], 16 * (n - h))
                    ch = Chain(dve, s_x2, 2 * n)
                    ch.then(nc.vector.tensor_tensor(x_new[:, h], x[:, h], fo[:, h, :, 0:D], ALU.add))
                    ch.then(nc.vector.tensor_scalar(sign[:], nt[:, h], -2.0, 1.0, ALU.mult, ALU.add))
                    norm(n, x_new[:, h], h2[:, h], s_res, sign[:])
                    dve.sem_inc(s_free, 1)
                else:
                    dve.wait_ge(s_a, n + 1)
                    dve.sem_inc(s_free, 1)

            if last:
                s_x2 = sem("x2_chain")
            if first:
                lagged(dve, ND, prep, main)
            else:
                with dve.Fori(0, ND // 2) as i:
                    for h in range(2):
                        main(2 * i + h, h)
    release(nc, sems)


def attention_logits(nc, m):
    G14 = NP_ // (NG * P)
    sems = []

    def keep(s):
        sems.append(s)
        return s

    with ExitStack() as ctx:
        def sb(name, shape, dt=F32):
            return ctx.enter_context(nc.sbuf_tensor(f"al_{name}", shape, dt))

        def sem(name):
            return keep(nc.alloc_semaphore(f"logits_{name}"))

        idx = sb("idx", [P, RING, 2, U], I32)
        g = sb("g", [P, RING, 2, U, D])
        cen = sb("cen", [P, 2 * U, D])
        sq = sb("sq", [P, 2 * U, D])
        stat = sb("stat", [P, 5, 2 * U])
        hn = sb("hn", [P, RING, 2, U, D])
        dots = sb("dots", [P, 2 * U])
        x = sb("x", [P, RING, G14, D])
        y = sb("y", [P, RING, G14, D])
        s_init = sem("init")
        s_tick = sem("tick")
        s_idx = sem("indices_staged")
        s_g = [sem(f"gathered{k}") for k in range(RING)]
        s_ln = sem("norm_chain")
        s_cen = sem("centered")
        s_sq = sem("squared")
        s_dev = sem("deviation")
        s_h = sem("rows_normed")
        s_hs = [sem(f"rows_stored{k}") for k in range(RING)]
        s_x = [sem(f"x_loaded{k}") for k in range(RING)]
        s_y = sem("x_and_bias")
        s_out = [sem(f"out_stored{k}") for k in range(RING)]
        block = ctx.enter_context(nc.Block())

        @block.sync
        def _(sp):
            xv = m.x.rearrange("(n p k) d -> n p (k d)", p=P, k=G14)

            def load(n, h):
                sp.wait_ge(s_y, n + 1)
                settle(sp, s_tick)
                sp.dma_start(x[:, h].rearrange("p k d -> p (k d)"), xv[bass.ds(n, 1)].rearrange("o p f -> (o p) f")).then_inc(s_x[h], 16)

            def store(n, h):
                sp.wait_ge(s_h, n + 1)
                settle(sp, s_tick)
                sp.dma_start(m.h3[:, bass.ds(tile_base(n), U), :], hn[:, h, 0]).then_inc(s_hs[h], 16)
                sp.wait_ge(s_y, n + 1 + RING)
                settle(sp, s_tick)
                if isinstance(n, int) and n == NG - 1:
                    first = n * P * G14
                    full = (N - first) // G14
                    tail = N - first - full * G14
                    sp.dma_start(m.out[first:first + full * G14].rearrange("(p k) d -> p (k d)", k=G14),
                                 y[0:full, h].rearrange("p k d -> p (k d)")).then_inc(s_out[h], 16)
                    sp.dma_start(m.out[N - tail:N].rearrange("(o k) d -> o (k d)", o=1),
                                 y[full:full + 1, h, 0:tail].rearrange("p k d -> p (k d)")).then_inc(s_out[h], 16)
                else:
                    o = m.out[0:(NG - 1) * P * G14].rearrange("(n p k) d -> n p (k d)", p=P, k=G14)
                    sp.dma_start(o[bass.ds(n, 1)].rearrange("o p f -> (o p) f"), y[:, h].rearrange("p k d -> p (k d)")).then_inc(s_out[h], 16)

            lagged(sp, NG, load, store)
            for h in range(RING):
                sp.wait_ge(s_hs[h], 16 * (NG // 2))
                sp.wait_ge(s_out[h], 16 * (NG // 2 + h))

        @block.gpsimd
        def _(pool):
            limit = pool.to_reg(N - 1)

            def fetch(n, h):
                pool.wait_ge(s_idx, n + 1)
                settle(pool, s_tick)
                for a in range(2):
                    for k in range(U):
                        nc.gpsimd.indirect_dma_start(
                            out=g[:, h, a, k, :], out_offset=None, in_=m.x,
                            in_offset=bass.IndirectOffsetOnAxis(ap=idx[:, h, a, k:k + 1], axis=0),
                            bounds_check=limit, oob_is_err=False).then_inc(s_g[h], 16)

            with pool.Fori(0, NG // 2) as i:
                for h in range(2):
                    fetch(2 * i + h, h)

        @block.scalar
        def _(act):
            with act.Fori(0, NG // 2) as i:
                for h in range(2):
                    n = 2 * i + h
                    act.wait_ge(s_cen, n + 1)
                    nc.scalar.activation(sq[:], cen[:], ACT.Square).then_inc(s_sq, 1)
                    act.wait_ge(s_dev, 2 * n + 1)
                    nc.scalar.activation(stat[:, 2, :], stat[:, 1, :], ACT.Sqrt, bias=m.eps[:, 0:1], scale=1.0 / D).then_inc(s_dev, 1)

        @block.vector
        def _(dve):
            nc.vector.memset(g[:], 0.0).then_inc(s_init, 1)
            dve.wait_ge(s_init, 1)
            dve.sem_inc(s_y, RING)
            for n in range(RING):
                nc.vector.tensor_copy(idx[:, n, 0, :], m.src_i[:, FRONT + tile_base(n):FRONT + tile_base(n) + U])
                nc.vector.tensor_copy(idx[:, n, 1, :], m.dst_i[:, FRONT + tile_base(n):FRONT + tile_base(n) + U]).then_inc(s_idx, 1)
            with dve.Fori(0, NG // 2) as i:
                for h in range(2):
                    n = 2 * i + h
                    dve.wait_ge(s_g[h], 32 * U * i + 32 * U)
                    ch = Chain(dve, s_ln, 6 * n)
                    rows = g[:, h].rearrange("p a k d -> p (a k) d")
                    ch.then(nc.vector.tensor_reduce(stat[:, 0, :], rows, AX.X, ALU.add))
                    nc.vector.scalar_tensor_tensor(out=cen[:], in0=bc(stat[:, 0, :], 2, [P, 2 * U, D]), scalar=-1.0 / D,
                                                   in1=rows, op0=ALU.mult, op1=ALU.add).then_inc(s_cen, 1)
                    dve.wait_ge(s_x[h], 16 * i + 16)
                    dve.wait_ge(s_out[h], 16 * i)
                    nc.vector.tensor_tensor(y[:, h], x[:, h], bc(m.bias3[:], 1, [P, G14, D]), ALU.add).then_inc(s_y, 1)
                    dve.wait_ge(s_sq, n + 1)
                    nc.vector.tensor_copy(idx[:, h, 0, :], m.src_i[:, bass.ds(FRONT + tile_base(n + 2), U)])
                    nc.vector.tensor_copy(idx[:, h, 1, :], m.dst_i[:, bass.ds(FRONT + tile_base(n + 2), U)]).then_inc(s_idx, 1)
                    nc.vector.tensor_reduce(stat[:, 1, :], sq[:], AX.X, ALU.add).then_inc(s_dev, 1)
                    dve.wait_ge(s_dev, 2 * n + 2)
                    ch.then(nc.vector.reciprocal(stat[:, 3, :], stat[:, 2, :]))
                    dve.wait_ge(s_hs[h], 16 * i)
                    both = hn[:, h].rearrange("p a k d -> p (a k) d")
                    nc.vector.scalar_tensor_tensor(out=both, in0=cen[:], scalar=0.0, in1=bc(stat[:, 3, :], 2, [P, 2 * U, D]),
                                                   op0=ALU.max, op1=ALU.mult).then_inc(s_h, 1)
                    dve.wait_ge(s_h, n + 1)
                    nc.vector.tensor_tensor(cen[:, 0:U], hn[:, h, 0], bc(m.wl[:], 1, [P, U, D]), ALU.mult)
                    ch.then(nc.vector.tensor_tensor(cen[:, U:2 * U], hn[:, h, 1], bc(m.wr[:], 1, [P, U, D]), ALU.mult))
                    ch.then(nc.vector.tensor_reduce(dots[:], cen[:], AX.X, ALU.add))
                    ch.then(nc.vector.tensor_tensor(stat[:, 4, 0:U], dots[:, 0:U], dots[:, U:2 * U], ALU.add))
                    ch.then(nc.vector.scalar_tensor_tensor(out=m.e_t[:, bass.ds(tile_base(n), U)], in0=stat[:, 4, 0:U], scalar=0.2,
                                                   in1=stat[:, 4, 0:U], op0=ALU.mult, op1=ALU.max))
    release(nc, sems)


def attention_weights(nc, m):
    sems = []

    def keep(s):
        sems.append(s)
        return s

    with ExitStack() as ctx:
        def sb(name, shape, dt=F32):
            return ctx.enter_context(nc.sbuf_tensor(f"aw_{name}", shape, dt))

        def ps(name, shape):
            return ctx.enter_context(nc.psum_tensor(f"aw_{name}", shape, F32))

        e = sb("e", [R, CH, P])
        gate_f = sb("gate_f", [R, CH, P])
        gate_b = sb("gate_b", [R, CH, P])
        fwd = sb("fwd", [R, CH, P])
        bwd = sb("bwd", [R, CH, P])
        thru = sb("thru", [R, 2, CH])
        ends = sb("ends", [1, 4, T])
        run = sb("run", [1, 2, T + 1])
        carry = sb("carry", [R, 2, CH])
        p_e = ps("p_e", [R, CH * P])
        p_ends = [ps(f"p_ends{k}", [1, 512]) for k in range(4)]
        p_carry = ps("p_carry", [R, 2 * CH])
        p_back = ps("p_back", [P, 512])
        s_c = keep(nc.alloc_semaphore("weights_chain"))
        s_t = keep(nc.alloc_semaphore("weights_turned"))
        s_d = keep(nc.alloc_semaphore("weights_rows_ready"))
        s_x = keep(nc.alloc_semaphore("weights_exp"))
        block = ctx.enter_context(nc.Block())

        @block.tensor
        def _(pe):
            for c in range(CH):
                mm = pe.transpose(p_e[:, c * P:(c + 1) * P], m.e_t[:, c * R:(c + 1) * R], m.ident[:])
            mm.then_inc(s_t, 1)
            pe.wait_ge(s_d, 1)
            for c in range(CH):
                cols = slice(c * R, (c + 1) * R)
                pe.transpose(p_ends[0][:, cols], fwd[:, c, P - 1:P], m.ident[0:R, 0:R])
                pe.transpose(p_ends[1][:, cols], bwd[:, c, 0:1], m.ident[0:R, 0:R])
                pe.transpose(p_ends[2][:, cols], thru[:, 0, c:c + 1], m.ident[0:R, 0:R])
                mm = pe.transpose(p_ends[3][:, cols], thru[:, 1, c:c + 1], m.ident[0:R, 0:R])
            mm.then_inc(s_t, 1)
            pe.wait_ge(s_d, 2)
            for c in range(CH):
                pe.transpose(p_carry[:, c:c + 1], run[:, 0, c * R:(c + 1) * R], m.ident[0:1, 0:1])
                mm = pe.transpose(p_carry[:, CH + c:CH + c + 1], run[:, 1, c * R + 1:(c + 1) * R + 1], m.ident[0:1, 0:1])
            mm.then_inc(s_t, 1)
            pe.wait_ge(s_x, 1)
            for c in range(CH):
                mm = pe.transpose(p_back[:, c * R:(c + 1) * R], e[:, c, :], m.ident[0:R, 0:R])
            mm.then_inc(s_t, 1)

        @block.scalar
        def _(act):
            act.wait_ge(s_d, 3)
            nc.scalar.activation(e[:], bwd[:], ACT.Exp).then_inc(s_x, 1)

        @block.vector
        def _(dve):
            ch = Chain(dve, s_c, 0)
            dst = m.dst_f
            nc.vector.tensor_tensor(gate_f[:, :, 1:P], dst[:, :, 1:P], dst[:, :, 0:P - 1], ALU.is_equal)
            nc.vector.tensor_tensor(gate_f[:, :, 0], dst[:, :, 0], m.before[:], ALU.is_equal)
            nc.vector.tensor_tensor(gate_b[:, :, 0:P - 1], dst[:, :, 1:P], dst[:, :, 0:P - 1], ALU.is_equal)
            nc.vector.tensor_tensor(gate_b[:, :, P - 1], dst[:, :, P - 1], m.after[:], ALU.is_equal)
            nc.vector.tensor_tensor(thru[:, 0, :], dst[:, :, P - 1], m.before[:], ALU.is_equal)
            ch.then(nc.vector.tensor_tensor(thru[:, 1, :], dst[:, :, 0], m.after[:], ALU.is_equal))
            for t in (gate_f, gate_b, thru):
                ins_ = nc.vector.tensor_scalar(t[:], t[:], -1.0, BIG, ALU.add, ALU.mult)
            ch.then(ins_)
            nc.vector.memset(run[:], -BIG)
            dve.wait_ge(s_t, 1)
            ch.then(nc.vector.tensor_copy(e[:].rearrange("r c p -> r (c p)"), p_e[:]))
            for c in range(CH):
                nc.vector.tensor_tensor_scan(fwd[:, c, :], gate_f[:, c, :], e[:, c, :], -BIG, ALU.add, ALU.max)
                ins_ = nc.vector.tensor_tensor_scan(bwd[:, c, ::-1], gate_b[:, c, ::-1], e[:, c, ::-1], -BIG, ALU.add, ALU.max)
            ins_.then_inc(s_d, 1)
            dve.wait_ge(s_t, 2)
            for k in range(4):
                ins_ = nc.vector.tensor_copy(ends[:, k, :], p_ends[k][:, 0:T])
            ch.then(ins_)
            nc.vector.tensor_tensor_scan(run[:, 0, 1:T + 1], ends[:, 2, :], ends[:, 0, :], -BIG, ALU.add, ALU.max)
            nc.vector.tensor_tensor_scan(run[:, 1, T - 1::-1], ends[:, 3, ::-1], ends[:, 1, ::-1], -BIG, ALU.add, ALU.max).then_inc(s_d, 1)
            dve.wait_ge(s_t, 3)
            ch.then(nc.vector.tensor_copy(carry[:].rearrange("r a c -> r (a c)"), p_carry[:]))
            nc.vector.tensor_tensor(gate_f[:], dst[:], bc(m.before[:], 2, [R, CH, P]), ALU.is_equal)
            ch.then(nc.vector.tensor_tensor(gate_b[:], dst[:], bc(m.after[:], 2, [R, CH, P]), ALU.is_equal))
            nc.vector.tensor_scalar(gate_f[:], gate_f[:], -1.0, BIG, ALU.add, ALU.mult)
            ch.then(nc.vector.tensor_scalar(gate_b[:], gate_b[:], -1.0, BIG, ALU.add, ALU.mult))
            nc.vector.tensor_tensor(gate_f[:], gate_f[:], bc(carry[:, 0, :], 2, [R, CH, P]), ALU.add)
            ch.then(nc.vector.tensor_tensor(gate_b[:], gate_b[:], bc(carry[:, 1, :], 2, [R, CH, P]), ALU.add))
            nc.vector.tensor_tensor(fwd[:], fwd[:], gate_f[:], ALU.max)
            ch.then(nc.vector.tensor_tensor(bwd[:], bwd[:], gate_b[:], ALU.max))
            ch.then(nc.vector.tensor_tensor(fwd[:], fwd[:], bwd[:], ALU.max))
            nc.vector.tensor_tensor(bwd[:], e[:], fwd[:], ALU.subtract).then_inc(s_d, 1)
            dve.wait_ge(s_t, 4)
            ch.then(nc.vector.tensor_copy(m.e_t[:], p_back[:, 0:T]))
    release(nc, sems)


def build(nc, ins, out, stages=99):
    with ExitStack() as ctx:
        m = allocate(nc, ctx, ins, out)
        halves = [fa.rearrange("n (a d) -> (n a) d", a=2) for fa in m.fa]
        todo = [lambda: set_up(nc, m),
                lambda: edge_round(nc, m, "sum", ins["x"], m.x),
                lambda: edge_round(nc, m, "first", m.x, m.a0),
                lambda: dense_step(nc, m, 0, None, m.fa[0]),
                lambda: edge_round(nc, m, "step", halves[0], halves[0]),
                lambda: dense_step(nc, m, 1, m.fa[0], m.fa[1]),
                lambda: edge_round(nc, m, "step", halves[1], halves[1]),
                lambda: dense_step(nc, m, 2, m.fa[1], m.fa[2]),
                lambda: edge_round(nc, m, "step", halves[2], halves[2]),
                lambda: dense_step(nc, m, 3, m.fa[2], None),
                lambda: edge_round(nc, m, "typed", m.h2, m.x),
                lambda: attention_logits(nc, m),
                lambda: attention_weights(nc, m),
                lambda: edge_round(nc, m, "attend", None, out)]
        for stage in todo[:stages]:
            stage()


INPUTS = ["x", "src", "dst", "edge_attr_32", "edge_type_3", "edge_type_4", "edge_weight", "node_type_2",
          "L1_gnn_W", "L1_gnn_b", "L1_gnn_w_ih", "L1_gnn_w_hh", "L1_gnn_b_ih", "L1_gnn_b_hh",
          "L2_gnn_W_node", "L2_gnn_W_msg", "L3_gnn_W", "L3_gnn_attn_l", "L3_gnn_attn_r", "L3_gnn_bias"]


def kernel(**inputs):
    import numpy as _np
    import concourse.bacc as _bacc
    from concourse.bass_utils import run_bass_kernel_spmd as _run

    nc = _bacc.Bacc("TRN2", target_bir_lowering=False, num_devices=1)
    arrays, aps = {}, {}
    for name in INPUTS:
        a = _np.ascontiguousarray(inputs[name])
        arrays[f"in_{name}"] = a
        aps[name] = nc.dram_tensor(f"in_{name}", a.shape, mybir.dt.from_np(a.dtype), kind="ExternalInput").ap()
    out = nc.dram_tensor("out_0", (N, D), F32, kind="ExternalOutput").ap()
    build(nc, aps, out)
    r = _run(nc, [arrays], core_ids=[0])
    return r.results[0]["out_0"]
```

```python
from contextlib import ExitStack

import concourse.bass as bass
from concourse import mybir

F32 = mybir.dt.float32
BF16 = mybir.dt.bfloat16
I32 = mybir.dt.int32
ALU = mybir.AluOpType
ACT = mybir.ActivationFunctionType
AX = mybir.AxisListType

P = 128
D = 64
N = 100000
E = 50000
U = 7
T = 392
NG = T // U
EP = T * P
FRONT = 2 * U
CH = 4
R = T // CH
GD = 28
ND = 28
NP_ = ND * GD * P
Q = 4
NQ = GD // Q
FAR = float(1 << 20)
BIG = 1e30
EPS = 1e-5
RING = 2


def tile_base(n):
    return T - U * (n + 1)


def lagged(eng, count, prep, main):
    prep(0, 0)
    with eng.Fori(0, count // 2 - 1) as i:
        for h in range(2):
            prep(2 * i + h + 1, 1 - h)
            main(2 * i + h, h)
    prep(count - 1, 1)
    main(count - 2, 0)
    main(count - 1, 1)


def pairs(eng, count, unit):
    unit(0, 0)
    unit(1, 1)
    with eng.Fori(1, count // 2 - 1) as i:
        for h in range(2):
            unit(2 * i + h, h)
    unit(count - 2, 0)
    unit(count - 1, 1)


def is_below(n, count):
    return isinstance(n, int) and n < count


def is_from(n, first):
    return isinstance(n, int) and n >= first


class Chain:

    def __init__(self, eng, sem, first):
        self.eng, self.sem, self.value = eng, sem, first

    def then(self, ins):
        ins.then_inc(self.sem, 1)
        self.value = self.value + 1
        self.eng.wait_ge(self.sem, self.value)


def bc(ap, axis, shape):
    return ap.unsqueeze(axis).to_broadcast(shape)


def settle(eng, tick):
    eng.sem_inc(tick, 1)


def release(nc, sems):
    nc.clear_and_free_semaphores(sems)
    nc.all_engine_barrier()


class Mem:
    pass


def allocate(nc, ctx, ins, out):
    m = Mem()

    def sb(name, shape, dt):
        return ctx.enter_context(nc.sbuf_tensor(name, shape, dt))

    def dram(name, shape, dt):
        return nc.dram_tensor(name, shape, dt, kind="Internal").ap()

    m.ins, m.out = ins, out
    m.s_all = sb("s_all", [P, T * P], BF16)
    m.src_i = sb("src_i", [P, FRONT + T], I32)
    m.dst_i = sb("dst_i", [P, FRONT + T], I32)
    m.row_i = sb("row_i", [P, FRONT + T], I32)
    m.src2_i = sb("src2_i", [P, FRONT + T], I32)
    m.row2_i = sb("row2_i", [P, FRONT + T], I32)
    m.dst_t = sb("dst_t", [P, T], F32)
    m.ew_t = sb("ew_t", [P, T], F32)
    m.em4 = sb("em4", [P, T, 4], F32)
    m.em3 = sb("em3", [P, T, 3], F32)
    m.dst_f = sb("dst_f", [R, CH, P], F32)
    m.before = sb("before", [R, CH], F32)
    m.after = sb("after", [R, CH], F32)
    m.e_t = sb("e_t", [P, T], F32)
    m.ident = sb("ident", [P, P], F32)
    m.w_gru = sb("w_gru", [P, 4 * D], F32)
    m.b_gru = sb("b_gru", [P, 2, 4 * D], BF16)
    m.ones3 = sb("ones3", [P, P], BF16)
    m.w_msg1 = sb("w_msg1", [P, 2, D], F32)
    m.b_msg1 = sb("b_msg1", [P, D], F32)
    m.w_node = sb("w_node", [P, D], F32)
    m.w_msg2 = sb("w_msg2", [96, 3, D], F32)
    m.w_att = sb("w_att", [D, D], F32)
    m.wl = sb("wl", [P, D], F32)
    m.wr = sb("wr", [P, D], F32)
    m.bias3 = sb("bias3", [P, D], F32)
    m.eps = sb("eps", [P, 1], F32)
    m.x = dram("x_work", [NP_, D], F32)
    m.fa = dram("f_and_a", [NP_, 2 * D], F32)
    m.h2 = dram("h2_signed", [NP_, D], F32)
    m.nt = dram("node_type_padded", [NP_], I32)
    m.attr = dram("edge_attr_padded", [EP, 32], F32)
    m.dst_rows = dram("dst_rows", [T + 2, P], F32)
    m.cx = dram("carry_rows", [5, EP], F32)
    m.h3 = dram("h3_by_edge", [P, T, D], F32)
    return m


def set_up(nc, m):
    ins = m.ins
    KZ = 8
    sems = []

    def keep(s):
        sems.append(s)
        return s

    with ExitStack() as ctx:
        def sb(name, shape, dt):
            return ctx.enter_context(nc.sbuf_tensor(name, shape, dt))

        def ps(name, shape):
            return ctx.enter_context(nc.psum_tensor(name, shape, F32))

        def sem(name):
            return keep(nc.alloc_semaphore(name))

        raw = sb("raw", [R, 5, CH, P], I32)
        flat = sb("flat", [R, 5, CH, P], F32)
        prev = sb("prev", [R, CH, P], F32)
        same = sb("same", [R, CH, P], F32)
        tab = sb("tab", [P, 6, T], F32)
        zero = sb("zero", [P, KZ * D], F32)
        izero = sb("izero", [P, 16], I32)
        minus = sb("minus", [2, P], F32)
        wl_rz = sb("wl_rz", [P, P], F32)
        wl_h = sb("wl_h", [D, P], F32)
        wl_i = sb("wl_i", [D, P], F32)
        wl_1 = sb("wl_1", [D, 4, D], F32)
        brow = sb("brow", [3, 2, 4 * D], F32)
        bh = sb("bh", [3, 4, 4 * D], F32)
        bpart = sb("bpart", [3, 3, 4 * D], BF16)
        att = sb("att", [D, 2], F32)
        att_b = sb("att_b", [D, 2, P], F32)
        w_attT = sb("w_attT", [D, D], F32)
        iota4 = sb("iota4", [P, 4], F32)
        dbc = sb("dbc", [P, RING, U * P], F32)
        oh = sb("oh", [P, RING, U, 4], BF16)
        cnt = sb("cnt", [4, RING, U * P], F32)
        pt = [ps(f"su_pt{k}", [P, 512]) for k in range(2)]
        pw = ps("su_pw", [P, 512])
        pv = ps("su_pv", [P, 512])
        pc = [ps(f"su_pc{k}", [4, 1024]) for k in range(2)]

        s_fill = sem("su_fill")
        s_tick = sem("su_tick")
        s_edges = sem("su_edges")
        s_w = sem("su_weights")
        s_copy = sem("su_copies")
        s_minus = sem("su_minus")
        s_id = sem("su_ident")
        s_dve = sem("su_dve")
        s_flat = sem("su_flat")
        s_rows = sem("su_dst_rows")
        s_nxt = sem("su_next")
        s_same = sem("su_same")
        s_pt = sem("su_turned")
        s_tab = sem("su_tab")
        s_wt = sem("su_w_turned")
        s_wc = sem("su_w_copied")
        s_prev = sem("su_prev")
        s_zero = sem("su_zero")
        s_parts = sem("su_bias_parts")
        s_bias = sem("su_bias_rows")
        s_dbc = [sem(f"su_dbc{k}") for k in range(RING)]
        s_s = sem("su_s")
        s_pc = sem("su_counts")
        s_cnt = sem("su_counts_copied")
        s_cx = [sem(f"su_cx{k}") for k in range(RING)]
        names = ("dst", "src", "edge_type_4", "edge_type_3", "edge_weight")
        full = 3 * R
        rest = E // P - full
        tail = E - (full + rest) * P
        block = ctx.enter_context(nc.Block())

        @block.sync
        def _(sp):
            sp.wait_ge(s_fill, 1)
            for a, name in enumerate(names):
                src = ins[name]
                to = raw if a < 4 else flat
                sp.dma_start(to[:, a, 0:3, :], src[0:full * P].rearrange("(c r p) -> r c p", c=3, p=P)).then_inc(s_edges, 16)
                sp.dma_start(to[0:rest, a, 3, :], src[full * P:(full + rest) * P].rearrange("(r p) -> r p", p=P)).then_inc(s_edges, 16)
                sp.dma_start(to[rest:rest + 1, a, 3, 0:tail], src[(full + rest) * P:E].rearrange("(o p) -> o p", o=1)).then_inc(s_edges, 16)
            sp.dma_start(wl_rz[:, 0:D], ins["L1_gnn_w_hh"][0:P]).then_inc(s_w, 16)
            sp.dma_start(wl_rz[:, D:P], ins["L1_gnn_w_ih"][0:P]).then_inc(s_w, 16)
            sp.dma_start(wl_h[:, 0:D], ins["L1_gnn_w_hh"][P:P + D]).then_inc(s_w, 16)
            sp.dma_start(wl_i[:, D:P], ins["L1_gnn_w_ih"][P:P + D]).then_inc(s_w, 16)
            sp.dma_start(wl_1[:], ins["L1_gnn_W"].rearrange("k h d -> h k d")).then_inc(s_w, 16)
            sp.dma_start(m.b_msg1[1:5, :], ins["L1_gnn_b"]).then_inc(s_w, 16)
            sp.dma_start(brow[:, 0, 0:3 * D], ins["L1_gnn_b_hh"].rearrange("(o n) -> o n", o=1).to_broadcast([3, 3 * D])).then_inc(s_w, 16)
            sp.dma_start(brow[:, 1, 0:3 * D], ins["L1_gnn_b_ih"].rearrange("(o n) -> o n", o=1).to_broadcast([3, 3 * D])).then_inc(s_w, 16)
            sp.dma_start(m.w_node[:], ins["L2_gnn_W_node"].rearrange("t k n -> (t k) n")).then_inc(s_w, 16)
            sp.dma_start(m.w_msg2[:], ins["L2_gnn_W_msg"].rearrange("t k n -> k t n")).then_inc(s_w, 16)
            sp.dma_start(m.w_att[:], ins["L3_gnn_W"]).then_inc(s_w, 16)
            sp.dma_start(att[:, 0:1], ins["L3_gnn_attn_l"].rearrange("(d o) -> d o", o=1)).then_inc(s_w, 16)
            sp.dma_start(att[:, 1:2], ins["L3_gnn_attn_r"].rearrange("(d o) -> d o", o=1)).then_inc(s_w, 16)
            sp.dma_start(m.bias3[:], ins["L3_gnn_bias"].rearrange("(o n) -> o n", o=1).to_broadcast([P, D])).then_inc(s_w, 16)
            sp.dma_start(m.dst_rows[0:T + 2:T + 1], minus[:]).then_inc(s_minus, 16)
            sp.wait_ge(s_flat, 1)
            sp.dma_start(m.dst_rows[1:T + 1].rearrange("(c r) p -> r c p", r=R), flat[:, 0]).then_inc(s_rows, 16)
            idle = (NP_ - N) // KZ
            sp.dma_start(m.x[N:NP_].rearrange("(p k) d -> p (k d)", k=KZ), zero[0:idle, :]).then_inc(s_copy, 16)
            sp.dma_start(m.nt[N:NP_].rearrange("(p k) -> p k", k=KZ), izero[0:idle, 0:KZ]).then_inc(s_copy, 16)
            sp.dma_start(m.attr[E:EP].rearrange("(p k) d -> p (k d)", p=16), zero[0:16, 0:11 * 32]).then_inc(s_copy, 16)
            sp.dma_start(m.x[0:N].rearrange("(a b c) d -> a b (c d)", a=16, b=25), ins["x"].rearrange("(a b c) d -> a b (c d)", a=16, b=25)).then_inc(s_copy, 16)
            sp.dma_start(m.nt[0:N].rearrange("(a b) -> a b", a=16), ins["node_type_2"].rearrange("(a b) -> a b", a=16)).then_inc(s_copy, 16)
            sp.dma_start(m.attr[0:E].rearrange("(a b) d -> a (b d)", a=80), ins["edge_attr_32"].rearrange("(a b) d -> a (b d)", a=80)).then_inc(s_copy, 16)
            sp.wait_ge(s_rows, 16)
            sp.wait_ge(s_minus, 16)
            with nc.allow_non_contiguous_dma(reason="one dst of each tile"):
                sp.dma_start(m.after[:], m.dst_rows[2:T + 2, 0].rearrange("(c r) -> r c", r=R)).then_inc(s_nxt, 16)
                sp.dma_start(m.before[:], m.dst_rows[0:T, P - 1].rearrange("(c r) -> r c", r=R)).then_inc(s_nxt, 16)
            sp.wait_ge(s_parts, 1)
            for k in range(3):
                sp.dma_start(m.b_gru[k:k + 1, 0, :], bpart[k:k + 1, k, :]).then_inc(s_bias, 16)
                sp.dma_start(m.b_gru[k:k + 1, 1, :], bpart[k:k + 1, k, :]).then_inc(s_bias, 16)
            sp.wait_ge(s_same, 1)
            sp.dma_start(m.cx[0].rearrange("(c r p) -> r c p", r=R, p=P), same[:]).then_inc(s_copy, 16)

            def load(n, h):
                sp.wait_ge(s_s, n + 1)
                settle(sp, s_tick)
                rows = m.dst_rows[bass.ds(tile_base(n) + 1, U)].rearrange("t p -> (t p)")
                sp.dma_start(dbc[:, h, :], bc(rows, 0, [P, U * P])).then_inc(s_dbc[h], 16)

            pairs(sp, NG, load)
            sp.wait_ge(s_edges, 16 * 15)
            sp.wait_ge(s_w, 16 * 14)
            sp.wait_ge(s_copy, 16 * 7)
            sp.wait_ge(s_nxt, 32)
            sp.wait_ge(s_bias, 16 * 6)

        @block.gpsimd
        def _(pool):
            nc.gpsimd.memset(m.ident[:], 0.0).then_inc(s_id, 1)
            nc.gpsimd.iota(iota4[:], [[1, 4]], base=0, channel_multiplier=0, allow_small_or_imprecise_dtypes=True).then_inc(s_id, 1)
            pool.wait_ge(s_id, 2)
            nc.gpsimd.affine_select(out=m.ident[:], in_=m.ident[:], compare_op=ALU.not_equal, fill=1.0, base=0,
                                    pattern=[[-1, P]], channel_multiplier=1).then_inc(s_id, 1)

        @block.tensor
        def _(pe):
            pe.wait_ge(s_id, 3)
            pe.wait_ge(s_flat, 1)
            for a in range(5):
                if a >= 2:
                    pe.wait_ge(s_tab, a - 1)
                for c in range(CH):
                    mm = pe.transpose(pt[a % 2][:, c * R:(c + 1) * R], flat[:, a, c, :], m.ident[0:R, 0:R])
                mm.then_inc(s_pt, 1)
            pe.wait_ge(s_tab, 4)
            pe.wait_ge(s_prev, 1)
            for c in range(CH):
                mm = pe.transpose(pt[1][:, c * R:(c + 1) * R], prev[:, c, :], m.ident[0:R, 0:R])
            mm.then_inc(s_pt, 1)
            pe.wait_ge(s_w, 16 * 14)
            pe.transpose(pw[:, 0:P], wl_rz[:], m.ident[:])
            pe.transpose(pw[:, P:P + D], wl_h[:], m.ident[0:D, 0:D])
            pe.transpose(pw[:, P + D:P + 2 * D], wl_i[:], m.ident[0:D, 0:D])
            for c in range(2):
                pe.transpose(pw[:, 4 * D + c * D:4 * D + (c + 1) * D], wl_1[:, 2 * c:2 * c + 2, :].rearrange("h k d -> h (k d)"), m.ident[0:D, 0:D])
            pe.transpose(pv[0:D, 0:D], m.w_att[:], m.ident[0:D, 0:D]).then_inc(s_wt, 1)
            pe.wait_ge(s_wc, 2)
            for a in range(2):
                mm = pe.matmul(pv[:, P + a * D:P + (a + 1) * D], lhsT=att_b[:, a, :], rhs=w_attT[:], start=True, stop=True)
            mm.then_inc(s_wt, 1)

            def counts(n, h):
                pe.wait_ge(s_s, n + 1 + RING)
                pe.wait_ge(s_cnt, n + 1)
                for k in range(U):
                    mm = pe.matmul(pc[h][:, k * P:(k + 1) * P], lhsT=oh[:, h, k, :],
                                   rhs=m.s_all[:, bass.ds((tile_base(n) + k) * P, P)], start=True, stop=True)
                mm.then_inc(s_pc, 1)

            with pe.Fori(0, NG // 2) as i:
                for h in range(2):
                    counts(2 * i + h, h)

        @block.scalar
        def _(act):
            act.sem_inc(s_cnt, RING)
            act.wait_ge(s_fill, 1)
            a0 = m.fa.rearrange("(g p k) d -> g p k d", p=P, k=KZ)
            with act.Fori(0, NP_ // (P * KZ)) as g:
                act.dma_start(a0[bass.ds(g, 1), :, :, D:2 * D].rearrange("o p k d -> (o p) k d"),
                              zero[:].rearrange("p (k d) -> p k d", k=KZ)).then_inc(s_zero, 16)
            def group(n, h):
                act.wait_ge(s_pc, n + 1)
                if not is_below(n, 2):
                    act.wait_ge(s_cx[h], 8 * (n - h))
                nc.scalar.copy(cnt[:, h, :], pc[h][:, 0:U * P]).then_inc(s_cnt, 1)
                act.wait_ge(s_cnt, n + 1 + RING)
                settle(act, s_tick)
                act.dma_start(m.cx[1:5, bass.ds(tile_base(n) * P, U * P)], cnt[:, h, :]).then_inc(s_cx[h], 16)

            pairs(act, NG, group)
            for h in range(RING):
                act.wait_ge(s_cx[h], 16 * (NG // 2))
            act.wait_ge(s_zero, 16 * (NP_ // (P * KZ)))

        @block.vector
        def _(dve):
            nc.vector.memset(raw[:, 0:2], int(FAR))
            nc.vector.memset(raw[:, 2:4], 0)
            nc.vector.memset(flat[:], 0.0)
            nc.vector.memset(zero[:], 0.0)
            nc.vector.memset(izero[:], 0)
            nc.vector.memset(minus[:], -1.0)
            nc.vector.memset(wl_h[:], 0.0)
            nc.vector.memset(wl_i[:], 0.0)
            nc.vector.memset(brow[:], 0.0)
            nc.vector.memset(m.b_msg1[:], 0.0)
            nc.vector.memset(m.b_gru[:], 0.0)
            nc.vector.memset(m.ones3[:], 0.0).then_inc(s_dve, 1)
            ch = Chain(dve, s_dve, 1)
            dve.wait_ge(s_dve, 1)
            ch.then(nc.vector.memset(m.ones3[0:3, :], 1.0))
            nc.vector.memset(m.eps[:], EPS)
            for t in (m.src_i, m.dst_i, m.row_i, m.src2_i, m.row2_i):
                nc.vector.memset(t[:, 0:FRONT], int(FAR))
            nc.vector.memset(prev[:], 0.0).then_inc(s_fill, 1)
            dve.wait_ge(s_edges, 16 * 15)
            ch.then(nc.vector.tensor_copy(flat[:, 0:4], raw[:, 0:4]))
            nc.vector.tensor_copy(m.dst_f[:], flat[:, 0])
            ch.then(nc.vector.tensor_copy(prev[:, :, 1:P], flat[:, 0, :, 0:P - 1]))
            dve.sem_inc(s_flat, 1)
            for a in range(5):
                dve.wait_ge(s_pt, a + 1)
                nc.vector.tensor_copy(tab[:, a, :], pt[a % 2][:, 0:T]).then_inc(s_tab, 1)
            dve.wait_ge(s_nxt, 32)
            nc.vector.tensor_tensor(same[:], flat[:, 0], bc(m.after[:], 2, [R, CH, P]), ALU.is_equal).then_inc(s_same, 1)
            nc.vector.tensor_copy(prev[:, :, 0], m.before[:]).then_inc(s_prev, 1)
            dve.wait_ge(s_pt, 6)
            nc.vector.tensor_copy(tab[:, 5, :], pt[1][:, 0:T]).then_inc(s_tab, 1)
            dve.wait_ge(s_tab, 6)
            dst, src = tab[:, 0, :], tab[:, 1, :]
            nc.vector.tensor_copy(m.dst_t[:], dst)
            nc.vector.tensor_copy(m.ew_t[:], tab[:, 4, :])
            nc.vector.tensor_copy(m.src_i[:, FRONT:], src)
            nc.vector.tensor_copy(m.dst_i[:, FRONT:], dst)
            nc.vector.tensor_scalar(m.src2_i[:, FRONT:], src, 2.0, None, ALU.mult)
            ch.then(nc.vector.tensor_tensor(tab[:, 5, :], tab[:, 5, :], dst, ALU.is_equal))
            ch.then(nc.vector.scalar_tensor_tensor(out=tab[:, 5, :], in0=tab[:, 5, :], scalar=FAR, in1=dst, op0=ALU.mult, op1=ALU.add))
            nc.vector.tensor_copy(m.row_i[:, FRONT:], tab[:, 5, :])
            nc.vector.tensor_scalar(m.row2_i[:, FRONT:], tab[:, 5, :], 2.0, 1.0, ALU.mult, ALU.add)
            for k in range(4):
                nc.vector.tensor_scalar(m.em4[:, :, k], tab[:, 2, :], float(k), None, ALU.is_equal)
            for k in range(3):
                ins_ = nc.vector.tensor_scalar(m.em3[:, :, k], tab[:, 3, :], float(k), None, ALU.is_equal)
            ch.then(ins_)
            dve.wait_ge(s_wt, 1)
            ch.then(nc.vector.tensor_copy(m.w_msg1[:].rearrange("p c d -> p (c d)"), pw[:, 4 * D:6 * D]))
            nc.vector.tensor_copy(m.w_gru[:, 0:4 * D], pw[:, 0:4 * D])
            nc.vector.tensor_copy(w_attT[:], pv[0:D, 0:D]).then_inc(s_wc, 1)
            nc.vector.tensor_copy(att_b[:], bc(att[:], 2, [D, 2, P])).then_inc(s_wc, 1)
            dve.wait_ge(s_wt, 2)
            nc.vector.tensor_copy(m.wl[:], pv[:, P:P + D])
            nc.vector.tensor_copy(m.wr[:], pv[:, P + D:P + 2 * D])
            ch.then(nc.vector.tensor_tensor(bh[:, 0, 0:2 * D], brow[:, 0, 0:2 * D], brow[:, 1, 0:2 * D], ALU.add))
            ch.then(nc.vector.tensor_copy(bh[:, 0, 2 * D:3 * D], brow[:, 0, 2 * D:3 * D]))
            ch.then(nc.vector.tensor_copy(bh[:, 0, 3 * D:4 * D], brow[:, 1, 2 * D:3 * D]))
            ch.then(nc.vector.tensor_copy(bpart[:, 0, :], bh[:, 0, :]))
            ch.then(nc.vector.tensor_tensor(bh[:, 1, :], bh[:, 0, :], bpart[:, 0, :], ALU.subtract))
            ch.then(nc.vector.tensor_copy(bpart[:, 1, :], bh[:, 1, :]))
            ch.then(nc.vector.tensor_tensor(bh[:, 2, :], bh[:, 1, :], bpart[:, 1, :], ALU.subtract))
            nc.vector.tensor_copy(bpart[:, 2, :], bh[:, 2, :]).then_inc(s_parts, 1)
            dve.sem_inc(s_s, RING)
            with dve.Fori(0, NG // 2) as i:
                for h in range(2):
                    n = 2 * i + h
                    dve.wait_ge(s_dbc[h], 16 * i + 16)
                    dve.wait_ge(s_cnt, n + 1)
                    nc.vector.tensor_copy(oh[:, h], m.em4[:, bass.ds(tile_base(n), U), :])
                    nc.vector.tensor_tensor(m.s_all[:, bass.ds(tile_base(n) * P, U * P)].rearrange("p (t s) -> p t s", t=U),
                                            dbc[:, h, :].rearrange("p (t s) -> p t s", t=U),
                                            bc(m.dst_t[:, bass.ds(tile_base(n), U)], 2, [P, U, P]), ALU.is_equal).then_inc(s_s, 1)
    release(nc, sems)


def edge_round(nc, m, kind, table=None, target=None):
    gather = kind != "attend"
    norm = kind in ("sum", "first")
    graph = kind in ("first", "step")
    W = D + 1 if kind == "attend" else D
    uid = nc.next_id()
    OC = U if graph else 1
    DONE = 2 * U
    sems = []

    def keep(s):
        sems.append(s)
        return s

    with ExitStack() as ctx:
        def sb(name, shape, dt=F32):
            return ctx.enter_context(nc.sbuf_tensor(f"{kind}{uid}_{name}", shape, dt))

        def ps(name, shape):
            return ctx.enter_context(nc.psum_tensor(f"{kind}{uid}_{name}", shape, F32))

        def sem(name):
            return keep(nc.alloc_semaphore(f"{kind}{uid}_{name}"))

        s_f32 = sb("s_f32", [P, RING, U * P])
        cx = sb("cx", [P, RING, U * P])
        if graph:
            car = sb("car", [P, RING, W])
        else:
            car = sb("car", [1, RING, U, W])
        o = sb("o", [P, RING, U, D])
        row_s = sb("row_s", [P, RING, U], I32)
        p_out = [ps(f"p_out{k}", [P, 512]) for k in range(RING)]
        if gather:
            idx = sb("idx", [P, RING, U], I32)
            g = sb("g", [P, RING, U, D])
        if norm:
            cen = sb("cen", [P, U, D])
            sq = sb("sq", [P, U, D])
            stat = sb("stat", [P, 4, U])
            msg = sb("msg", [P, RING, U, D])
        if graph:
            p_sum = [ps(f"p_sum{k}", [P, 512]) for k in range(RING)]
            agg = sb("agg", [P, RING, 2 * P])
            fm = sb("fm", [P, RING, U, 4, D])
        if kind == "typed":
            pos = sb("pos", [P, RING, U, 2, D])
            posT = sb("posT", [P, U * P])
            attr = sb("attr", [P, RING, U, D + 32])
            catT = sb("catT", [D + 32, U * P])
            sel = sb("sel", [P, U, 3, D])
            acc = sb("acc", [P, U, D])
            msg = sb("msg", [P, RING, U, D])
            p_turn = [ps(f"p_turn{k}", [P, 512]) for k in range(2)]
            p_b = ps("p_b", [P, 4, 512])
        if kind == "attend":
            h3 = sb("h3", [P, RING, U, D])
            msg = sb("msg", [P, RING, U, W])
            both = sb("both", [P, RING, U, W])
            den = sb("den", [P, 2, U])
            val = sb("val", [P, U, D])
            valT = sb("valT", [D, U * P])
            p_turn = [ps(f"p_turn{k}", [D, 512]) for k in range(2)]
            p_w = ps("p_w", [P, 512])

        s_init = sem("init")
        s_tick = sem("tick")
        s_idx = sem("indices_staged")
        s_g = [sem(f"gathered{k}") for k in range(RING)]
        s_cx = [sem(f"carry_rows{k}") for k in range(RING)]
        s_in = [sem(f"loaded{k}") for k in range(RING)]
        s_s = sem("s_ready")
        s_prep = sem("prep_chain")
        s_cen = sem("centered")
        s_sq = sem("squared")
        s_dev = sem("deviation")
        s_msg = sem("messages_ready")
        s_sum = sem("tiles_summed")
        s_part = sem("parts_summed")
        s_agg = sem("parts_copied")
        s_car = sem("carry_ready")
        s_o = sem("rows_ready")
        s_row = sem("row_indices")
        s_sc = [sem(f"scattered{k}") for k in range(RING)]
        s_t = sem("turned")
        s_tc = sem("turned_copied")
        s_x = sem("transformed")
        s_val = sem("values")
        s_w = sem("values_transformed")
        s_ready = sem("values_ready")
        s_cat = sem("cat_ready")
        s_pos = sem("both_signs")
        s_y = sem("typed_products")
        block = ctx.enter_context(nc.Block())
        src_i = m.src2_i if kind == "step" else m.src_i
        row_i = m.row2_i if graph else m.row_i
        read_bound = (2 * N if kind == "step" else N) - 1
        write_bound = (2 * N if graph else N) - 1


        typed = kind == "typed"
        SUMS, CARRIES, ADD, COPY = 1, 2, 3, 4

        def steps(eng, main, prep, post=None, close=None, ahead=None):
            def group(n, h):
                for j in range(U):
                    main(j, n, h)
                    if post and not is_below(n, 1):
                        post(j, n - 1, 1 - h)
                    if not is_from(n, NG - 1):
                        prep(j, n + 1, 1 - h)
                    if ahead and not is_from(n, NG - 2):
                        ahead(j, n + 2, h)
                if close:
                    close(n, h)

            for n in range(2 if ahead else 1):
                if ahead:
                    for j in range(U):
                        ahead(j, n, n)
                if n == 0:
                    for j in range(U):
                        prep(j, 0, 0)
            pairs(eng, NG, group)
            if post:
                for j in range(U):
                    post(j, NG - 1, 1)

        @block.sync
        def _(sp):
            sp.wait_ge(s_init, 1)

            def load_input(n, h):
                if kind == "typed":
                    view = m.attr.rearrange("(t p) f -> p t f", p=P)
                    sp.dma_start(attr[:, h, :, D:], view[:, bass.ds(tile_base(n), U), :]).then_inc(s_in[h], 16)
                if kind == "attend":
                    sp.dma_start(h3[:, h], m.h3[:, bass.ds(tile_base(n), U), :]).then_inc(s_in[h], 16)

            def group(n, h):
                if not is_from(n, NG - 1):
                    if not is_below(n, 1):
                        sp.wait_ge(s_msg, n)
                        settle(sp, s_tick)
                    load_input(n + 1, 1 - h)
                sp.wait_ge(s_sum, U * (n + 1))
                settle(sp, s_tick)
                rows_ = 5 if graph else 1
                sp.dma_start(cx[0:rows_, h, :], m.cx[0:rows_, bass.ds(tile_base(n) * P, U * P)]).then_inc(s_cx[h], 16)

            load_input(0, 0)
            pairs(sp, NG, group)

        @block.gpsimd
        def _(pool):
            read_limit, write_limit = pool.to_reg(read_bound), pool.to_reg(write_bound)

            def fetch(n, h):
                pool.wait_ge(s_idx, n + 1)
                settle(pool, s_tick)
                for k in range(U):
                    nc.gpsimd.indirect_dma_start(
                        out=g[:, h, k, :], out_offset=None, in_=table,
                        in_offset=bass.IndirectOffsetOnAxis(ap=idx[:, h, k:k + 1], axis=0),
                        bounds_check=read_limit, oob_is_err=False).then_inc(s_g[h], 16)

            def scatter(n, h):
                pool.wait_ge(s_row, n + 1)
                if kind == "attend":
                    pool.wait_ge(s_ready, n + 1)
                else:
                    pool.wait_ge(s_o, OC * (n + 1) + RING)
                settle(pool, s_tick)
                for k in range(U):
                    nc.gpsimd.indirect_dma_start(
                        out=target, out_offset=bass.IndirectOffsetOnAxis(ap=row_s[:, h, k:k + 1], axis=0),
                        in_=o[:, h, k, :], in_offset=None, bounds_check=write_limit, oob_is_err=False,
                        **({} if graph else {"compute_op": ALU.add})).then_inc(s_sc[h], 16)

            def group(n, h):
                if gather and not is_from(n, NG - 2):
                    fetch(n + 2, h)
                scatter(n, h)

            if gather:
                fetch(0, 0)
                fetch(1, 1)
            pairs(pool, NG, group)
            for h in range(RING):
                pool.wait_ge(s_sc[h], 16 * U * (NG // 2))

        @block.tensor
        def _(pe):
            pe.sem_inc(s_sum, DONE)
            pe.wait_ge(s_init, 1)

            def prep(j, n, h):
                if typed and j == 0:
                    pe.wait_ge(s_tc, n + 1)
                    if not is_below(n, 1):
                        pe.wait_ge(s_msg, n)
                    pe.matmul(p_b[0:D, 2, :], lhsT=m.w_node[:], rhs=posT[:, 0:4 * P], start=True, stop=True)
                    pe.matmul(p_b[0:D, 3, 0:3 * P], lhsT=m.w_node[:], rhs=posT[:, 4 * P:], start=True, stop=True)
                    pe.wait_ge(s_in[h], 8 * (n - h) + 16)
                    settle(pe, s_tick)
                    for k in range(U):
                        mm = pe.transpose(p_b[0:D + 32, k // 4, k % 4 * P:(k % 4 + 1) * P], attr[:, h, k, :], m.ident[:])
                    mm.then_inc(s_x, 1)
                if typed and j == 2:
                    pe.wait_ge(s_cat, n + 1)
                    for k in range(U):
                        mm = pe.matmul(p_b[:, k // 2, k % 2 * 3 * D:(k % 2 + 1) * 3 * D], lhsT=catT[:, k * P:(k + 1) * P],
                                       rhs=m.w_msg2[:].rearrange("p c d -> p (c d)"), start=True, stop=True)
                    mm.then_inc(s_y, 1)

            def ahead(j, n, h):
                if j == 5:
                    pe.wait_ge(s_pos, 2 * n + 2)
                    if not is_below(n, 1):
                        pe.wait_ge(s_tc, n)
                    settle(pe, s_tick)
                    for k in range(U):
                        mm = pe.transpose(p_turn[k // 4][:, k % 4 * P:(k % 4 + 1) * P],
                                          pos[:, h, k].rearrange("p a d -> p (a d)"), m.ident[:])
                    mm.then_inc(s_t, 1)

            def post(j, n, h):
                if j == 1:
                    pe.wait_ge(s_val, n + 1)
                    settle(pe, s_tick)
                    for k in range(U):
                        mm = pe.transpose(p_turn[k // 4][:, k % 4 * P:(k % 4 + 1) * P], val[:, k, :], m.ident[:])
                    mm.then_inc(s_t, 1)
                if j == 3:
                    pe.wait_ge(s_tc, n + 1)
                    if not is_below(n, 1):
                        pe.wait_ge(s_ready, n)
                    for k in range(U):
                        mm = pe.matmul(p_w[:, k * D:(k + 1) * D], lhsT=valT[:, k * P:(k + 1) * P], rhs=m.w_att[:], start=True, stop=True)
                    mm.then_inc(s_w, 1)

            def parts(q, h, k, slot):
                pe.wait_ge(s_agg, q + 1)
                for c in range(2):
                    lhs = fm[:, h, k, 2 * c:2 * c + 2, :].rearrange("p a d -> p (a d)")
                    mm = pe.matmul(p_sum[slot][:, c * P:(c + 1) * P], lhsT=lhs, rhs=s_f32[:, h, k * P:(k + 1) * P], start=True, stop=True)
                mm.then_inc(s_part, 1)

            def total(q, h, k, slot):
                pe.wait_ge(s_o, q + 1)
                to = p_out[slot][:, 0:W]
                pe.wait_ge(s_agg, q + 1 + RING)
                for c in range(2):
                    pe.matmul(to, lhsT=agg[:, slot, c * P:(c + 1) * P], rhs=m.w_msg1[:, c, :], start=(c == 0), stop=False)
                pe.wait_ge(s_car, q + 1)
                pe.matmul(to, lhsT=cx[:, h, k * P:(k + 1) * P], rhs=car[:, slot, :], start=False, stop=True).then_inc(s_sum, 1)

            def main(j, n, h):
                if j == (0 if graph else SUMS):
                    pe.wait_ge(s_msg, n + 1)
                    pe.wait_ge(s_s, n + 1)
                    pe.wait_ge(s_cx[h], 8 * (n - h) + 16)
                if graph:
                    parts(U * n + j, h, U - 1 - j, (U * h + j) % RING)
                    if j >= 1:
                        total(U * n + j - 1, h, U - j, (U * h + j - 1) % RING)
                elif j == SUMS:
                    own_sums(n, h)
                elif j == ADD:
                    add_carries(n, h)

            def own_sums(n, h):
                pe.wait_ge(s_o, n + 1)
                for k in range(U):
                    mm = pe.matmul(p_out[h][:, k * W:(k + 1) * W], lhsT=s_f32[:, h, k * P:(k + 1) * P], rhs=msg[:, h, k, :],
                                   start=(k == 0), stop=False, skip_group_check=True)
                mm.then_inc(s_part, 1)

            def add_carries(n, h):
                pe.wait_ge(s_car, U * (n + 1) + 1)
                for k in range(U):
                    pe.matmul(p_out[h][:, k * W:(k + 1) * W], lhsT=cx[0:1, h, k * P:(k + 1) * P], rhs=car[:, h, k, :],
                              start=False, stop=True, skip_group_check=True).then_inc(s_sum, 1)

            def close(n, h):
                total(U * n + U - 1, h, 0, (U * h + U - 1) % RING)

            steps(pe, main, prep, post if kind == "attend" else None, close if graph else None, ahead if typed else None)

        @block.scalar
        def _(act):
            if graph:
                act.sem_inc(s_agg, RING)

            def prep(j, n, h):
                if j == 0:
                    act.wait_ge(s_sum, U * (n + 1))
                    nc.scalar.copy(s_f32[:, h, :], m.s_all[:, bass.ds(tile_base(n) * P, U * P)]).then_inc(s_s, 1)
                if norm and j == 1:
                    act.wait_ge(s_cen, n + 1)
                    nc.scalar.activation(sq[:], cen[:], ACT.Square).then_inc(s_sq, 1)
                if norm and j == 3:
                    act.wait_ge(s_dev, 2 * n + 1)
                    nc.scalar.activation(stat[:, 2, :], stat[:, 1, :], ACT.Sqrt, bias=m.eps[:, 0:1], scale=1.0 / D).then_inc(s_dev, 1)
                if typed and j == 1:
                    act.wait_ge(s_x, n + 1)
                    if not is_below(n, 1):
                        act.wait_ge(s_y, n)
                    nc.scalar.copy(catT[0:D, 0:4 * P], p_b[0:D, 2, :])
                    nc.scalar.copy(catT[0:D, 4 * P:], p_b[0:D, 3, 0:3 * P])
                    nc.scalar.copy(catT[D:, 0:4 * P], p_b[D:D + 32, 0, :])
                    nc.scalar.copy(catT[D:, 4 * P:], p_b[D:D + 32, 1, 0:3 * P]).then_inc(s_cat, 1)

            def ahead(j, n, h):
                if j == 6:
                    act.wait_ge(s_t, n + 1)
                    if not is_below(n, 1):
                        act.wait_ge(s_x, n)
                    nc.scalar.copy(posT[:, 0:4 * P], p_turn[0][:])
                    nc.scalar.copy(posT[:, 4 * P:], p_turn[1][:, 0:3 * P]).then_inc(s_tc, 1)

            def main(j, n, h):
                q, slot = U * n + j, (U * h + j) % RING
                if graph:
                    act.wait_ge(s_part, q + 1)
                    act.wait_ge(s_sum, q + 1 + DONE - RING)
                    nc.scalar.copy(agg[:, slot, :], p_sum[slot][:, 0:2 * P]).then_inc(s_agg, 1)
                if not graph and j == COPY:
                    act.wait_ge(s_sum, U * (n + 1) + DONE)
                    if kind == "attend":
                        nc.scalar.copy(both[:, h].rearrange("p k w -> p (k w)"), p_out[h][:, 0:U * W]).then_inc(s_o, 1)
                    else:
                        if not is_below(n, 2):
                            act.wait_ge(s_sc[h], 8 * U * (n - h))
                        nc.scalar.copy(o[:, h].rearrange("p k d -> p (k d)"), p_out[h][:, 0:U * W]).then_inc(s_o, 1)

            def post(j, n, h):
                if j == 2:
                    act.wait_ge(s_t, n + 1)
                    nc.scalar.copy(valT[:, 0:4 * P], p_turn[0][:])
                    nc.scalar.copy(valT[:, 4 * P:], p_turn[1][:, 0:3 * P]).then_inc(s_tc, 1)
                if j == 4:
                    act.wait_ge(s_w, n + 1)
                    if not is_below(n, 2):
                        act.wait_ge(s_sc[h], 8 * U * (n - h))
                    nc.scalar.copy(o[:, h].rearrange("p k d -> p (k d)"), p_w[:, 0:U * D]).then_inc(s_ready, 1)

            steps(act, main, prep, post if kind == "attend" else None, ahead=ahead if typed else None)

        @block.vector
        def _(dve):
            nc.vector.memset(cx[:], 0.0)
            nc.vector.memset(car[:], 0.0).then_inc(s_car, 1)
            dve.wait_ge(s_car, 1)
            if gather:
                nc.vector.memset(g[:], 0.0)
            if kind == "typed":
                nc.vector.memset(attr[:, :, :, 0:D], 0.0)
            if graph:
                for slot in range(RING):
                    nc.vector.tensor_copy(car[:, slot, :], m.b_msg1[:])
            nc.vector.memset(o[:], 0.0).then_inc(s_init, 1)
            dve.wait_ge(s_init, 1)
            dve.sem_inc(s_o, RING)
            if gather:
                for n in range(RING):
                    nc.vector.tensor_copy(idx[:, n, :], src_i[:, FRONT + tile_base(n):FRONT + tile_base(n) + U]).then_inc(s_idx, 1)

            def refill(n, h):
                nc.vector.tensor_copy(idx[:, h, :], src_i[:, bass.ds(FRONT + tile_base(n + 2), U)]).then_inc(s_idx, 1)

            def prep(j, n, h):
                loads = 8 * (n - h) + 16
                tiles = bass.ds(tile_base(n), U)
                if gather and not typed and j == 0:
                    dve.wait_ge(s_g[h], U * loads)
                if norm and j == 0:
                    ch = Chain(dve, s_prep, 3 * n)
                    ch.then(nc.vector.tensor_reduce(stat[:, 0, :], g[:, h], AX.X, ALU.add))
                    nc.vector.scalar_tensor_tensor(out=cen[:], in0=bc(stat[:, 0, :], 2, [P, U, D]), scalar=-1.0 / D,
                                                   in1=g[:, h], op0=ALU.mult, op1=ALU.add).then_inc(s_cen, 1)
                if norm and j == 2:
                    dve.wait_ge(s_sq, n + 1)
                    refill(n, h)
                    nc.vector.tensor_reduce(stat[:, 1, :], sq[:], AX.X, ALU.add).then_inc(s_dev, 1)
                if norm and j == 4:
                    dve.wait_ge(s_dev, 2 * n + 2)
                    ch = Chain(dve, s_prep, 3 * n + 1)
                    ch.then(nc.vector.reciprocal(stat[:, 3, :], stat[:, 2, :]))
                    if kind == "sum":
                        ch.then(nc.vector.tensor_tensor(stat[:, 3, :], stat[:, 3, :], m.ew_t[:, tiles], ALU.mult))
                    dve.wait_ge(s_sum, U * (n + 1))
                    ins_ = nc.vector.scalar_tensor_tensor(out=msg[:, h], in0=cen[:], scalar=0.0, in1=bc(stat[:, 3, :], 2, [P, U, D]),
                                                          op0=ALU.max, op1=ALU.mult)
                    if kind == "sum":
                        ins_.then_inc(s_msg, 1)
                    else:
                        ch.then(ins_)
                if graph and j == (5 if norm else 0):
                    dve.wait_ge(s_sum, U * (n + 1))
                    settle(dve, s_tick)
                    rows_in = msg[:, h] if norm else g[:, h]
                    mask = m.em4[:, tiles, :]
                    nc.vector.tensor_tensor(fm[:, h], bc(rows_in, 2, [P, U, 4, D]), bc(mask, 3, [P, U, 4, D]), ALU.mult).then_inc(s_msg, 1)
                if kind == "step" and j == 1:
                    dve.wait_ge(s_msg, n + 1)
                    refill(n, h)
                if typed and j == 3:
                    dve.wait_ge(s_y, n + 1)
                    for b in range(4):
                        count = min(2, U - 2 * b)
                        y = p_b[:, b, 0:count * 3 * D].rearrange("p (k c d) -> p k c d", k=count, c=3)
                        mask = m.em3[:, bass.ds(tile_base(n) + 2 * b, count), :]
                        ins_ = nc.vector.tensor_tensor(sel[:, 2 * b:2 * b + count], y, bc(mask, 3, [P, count, 3, D]), ALU.mult)
                    ch = Chain(dve, s_prep, 2 * n)
                    ch.then(ins_)
                    ch.then(nc.vector.tensor_tensor(acc[:], sel[:, :, 0], sel[:, :, 1], ALU.add))
                    dve.wait_ge(s_sum, U * (n + 1))
                    nc.vector.tensor_tensor(msg[:, h], acc[:], sel[:, :, 2], ALU.add).then_inc(s_msg, 1)
                if kind == "attend" and j == 3:
                    dve.wait_ge(s_in[h], loads)
                    dve.wait_ge(s_sum, U * (n + 1))
                    settle(dve, s_tick)
                    e = m.e_t[:, tiles]
                    nc.vector.tensor_copy(msg[:, h, :, D:W].rearrange("p k o -> p (k o)"), e)
                    nc.vector.tensor_tensor(msg[:, h, :, 0:D], h3[:, h], bc(e, 2, [P, U, D]), ALU.mult).then_inc(s_msg, 1)

            def ahead(j, n, h):
                if j == 4:
                    dve.wait_ge(s_g[h], U * (8 * (n - h) + 16))
                    ch = Chain(dve, s_pos, 2 * n)
                    ch.then(nc.vector.tensor_scalar(pos[:, h, :, 0, :], g[:, h], 0.0, None, ALU.max))
                    ch.then(nc.vector.tensor_scalar(pos[:, h, :, 1, :], g[:, h], -1.0, 0.0, ALU.mult, ALU.max))
                    refill(n, h)

            def main(j, n, h):
                if j == (0 if graph else U - 1 if kind == "attend" else CARRIES + 1):
                    if not is_below(n, 2):
                        dve.wait_ge(s_sc[h], 8 * U * (n - h))
                    nc.vector.tensor_copy(row_s[:, h, :], row_i[:, bass.ds(FRONT + tile_base(n), U)]).then_inc(s_row, 1)
                if graph:
                    q, slot = U * n + j, (U * h + j) % RING
                    dve.wait_ge(s_sum, q + 1 + DONE)
                    nc.vector.tensor_copy(car[0:1, 1 - slot, :], p_out[slot][0:1, 0:W]).then_inc(s_car, 1)
                    nc.vector.tensor_copy(o[:, h, U - 1 - j, :], p_out[slot][:, 0:W]).then_inc(s_o, 1)
                elif j == CARRIES:
                    dve.wait_ge(s_cx[h], 8 * (n - h) + 16)
                    dve.wait_ge(s_part, n + 1)
                    dve.wait_ge(s_sum, U * n + DONE)
                    for k in range(U - 1, -1, -1):
                        dve.wait_ge(s_car, U * n + U - k)
                        to = car[:, h, k - 1, :] if k > 0 else car[:, 1 - h, U - 1, :]
                        nc.vector.scalar_tensor_tensor(out=to, in0=car[:, h, k, :], scalar=cx[0:1, h, k * P:k * P + 1],
                                                       in1=p_out[h][0:1, k * W:(k + 1) * W], op0=ALU.mult, op1=ALU.add).then_inc(s_car, 1)

            def post(j, n, h):
                if j == 0:
                    ch = Chain(dve, s_prep, 2 * n)
                    dve.wait_ge(s_o, OC * (n + 1) + RING)
                    total = both[:, h, :, D:W].rearrange("p k o -> p (k o)")
                    ch.then(nc.vector.scalar_tensor_tensor(out=den[:, 0, :], in0=total, scalar=0.0, in1=total, op0=ALU.is_equal, op1=ALU.add))
                    ch.then(nc.vector.reciprocal(den[:, 1, :], den[:, 0, :]))
                    if not is_below(n, 1):
                        dve.wait_ge(s_t, n)
                    nc.vector.tensor_tensor(val[:], both[:, h, :, 0:D], bc(den[:, 1, :], 2, [P, U, D]), ALU.mult).then_inc(s_val, 1)

            steps(dve, main, prep, post if kind == "attend" else None, ahead=ahead if typed else None)
    release(nc, sems)


def dense_step(nc, m, step):
    first, last = step == 0, step == 3
    NV = NQ * ND
    NP = 4
    PR = GD // NP
    sems = []

    def keep(s):
        sems.append(s)
        return s

    with ExitStack() as ctx:
        def sb(name, shape, dt=F32):
            return ctx.enter_context(nc.sbuf_tensor(f"d{step}_{name}", shape, dt))

        def sem(name):
            return keep(nc.alloc_semaphore(f"dense{step}_{name}"))

        fa = sb("fa", [P, RING, GD, 2 * D])
        faT = sb("faT", [P, RING, Q * P])
        rz = sb("rz", [P, RING, Q, 2 * D])
        tmp = sb("tmp", [P, RING, Q, D])
        pre = sb("pre", [P, RING, Q, D])
        cand = sb("cand", [P, RING, Q, D])
        dif = sb("dif", [P, RING, Q, D])
        new = sb("new", [P, RING, GD, D]) if not last else sb("new", [P, RING, Q, D])
        p_t = [ctx.enter_context(nc.psum_tensor(f"d{step}_pt{k}", [P, 512], F32)) for k in range(RING)]
        p_g = [ctx.enter_context(nc.psum_tensor(f"d{step}_pg{k}", [P, Q, 4 * D], F32)) for k in range(RING)]
        if first or last:
            x = sb("x", [P, RING, GD, D])
            stat = sb("stat", [P, 4, GD])
            half = sb("half", [P, GD])
        if last:
            sq = sb("sq", [P, GD, D])
            nt = sb("nt", [P, RING, GD], I32)
            sign = sb("sign", [P, GD])
            h2 = sb("h2", [P, GD, D])
        s_in = [sem(f"rows_loaded{k}") for k in range(RING)]
        s_x = [sem(f"x_loaded{k}") for k in range(RING)]
        s_out = [sem(f"rows_stored{k}") for k in range(RING)]
        s_h2 = [sem(f"h2_half{b}_stored") for b in range(2)]
        s_half = sem("exponents")
        s_zero = sem("zero_ready")
        s_table = sem("table_loaded")
        s_tick = sem("tick")
        s_t = sem("quads_turned")
        s_tc = sem("turned_copied")
        s_g = sem("gates")
        s_rz = sem("rz_ready")
        s_t1 = sem("r_times_h")
        s_pre = sem("pre_ready")
        s_cand = sem("cand_ready")
        s_dif = sem("differences")
        s_dz = sem("differences_times_z")
        s_upd = sem("quads_updated")
        s_new = sem("x_updated") if last else s_upd
        s_sum = sem("row_sums")
        s_cen = sem("units_centered")
        s_sq = sem("squares")
        s_sq2 = sem("square_sums")
        s_var = sem("variances")
        s_dev = sem("deviations")
        s_sign = sem("signed_deviations")
        s_f = sem("units_normed")
        block = ctx.enter_context(nc.Block())

        def unit_rows(ap, n):
            v = ap.rearrange("(g p k) d -> g p k d", p=P, k=GD)
            return v[bass.ds(n, 1)].rearrange("o p k d -> (o p) k d")

        def in_slot(n, h):
            return 8 * (n - h) + 16

        def squares(h):
            return x[:, h] if first else sq[:]

        @block.sync
        def _(sp):
            def load_rows(n, h):
                if first:
                    sp.dma_start(fa[:, h, :, D:2 * D], unit_rows(m.fa, n)[:, :, D:2 * D]).then_inc(s_in[h], 16)
                else:
                    sp.dma_start(fa[:, h], unit_rows(m.fa, n)).then_inc(s_in[h], 16)

            def load_x(n, h):
                sp.dma_start(x[:, h], unit_rows(m.x, n)).then_inc(s_x[h], 16)
                if last:
                    v = m.nt.rearrange("(g p k) -> g p k", p=P, k=GD)
                    sp.dma_start(nt[:, h], v[bass.ds(n, 1)].rearrange("o p k -> (o p) k")).then_inc(s_x[h], 16)

            def unit(n, h):
                start, end = is_below(n, 1), is_from(n, ND - 1)
                if first and not is_from(n, ND - 2):
                    sp.wait_ge(s_f, NP * (n + 1))
                    settle(sp, s_tick)
                    load_x(n + 2, h)
                if last and not is_below(n, 2):
                    store_h2(n - 2, 0)
                if not start:
                    sp.wait_ge(s_new, NQ * n)
                    settle(sp, s_tick)
                if not end:
                    load_rows(n + 1, 1 - h)
                if not start:
                    if last:
                        sp.dma_start(unit_rows(m.x, n - 1), x[:, 1 - h]).then_inc(s_out[1 - h], 16)
                    else:
                        sp.dma_start(unit_rows(m.fa, n - 1)[:, :, 0:D], new[:, 1 - h]).then_inc(s_out[1 - h], 16)
                if last and not is_below(n, 2):
                    store_h2(n - 2, 1)
                if last and not end:
                    if not start:
                        sp.wait_ge(s_cen, NP * n)
                        settle(sp, s_tick)
                        sp.wait_ge(s_out[1 - h], in_slot(n - 1, 1 - h))
                        settle(sp, s_tick)
                    load_x(n + 1, 1 - h)

            def store_h2(n, b):
                rows = slice(b * GD // 2, (b + 1) * GD // 2)
                sp.wait_ge(s_f, NP * n + NP // 2 * (b + 1))
                settle(sp, s_tick)
                sp.dma_start(unit_rows(m.h2, n)[:, rows], h2[:, rows]).then_inc(s_h2[b], 16)

            if first or last:
                load_x(0, 0)
            if first:
                load_x(1, 1)
            load_rows(0, 0)
            pairs(sp, ND, unit)
            sp.wait_ge(s_new, NV)
            if last:
                sp.dma_start(unit_rows(m.x, ND - 1), x[:, 1]).then_inc(s_out[1], 16)
                for n in (ND - 2, ND - 1):
                    for b in range(2):
                        store_h2(n, b)
            else:
                sp.dma_start(unit_rows(m.fa, ND - 1)[:, :, 0:D], new[:, 1]).then_inc(s_out[1], 16)
            for h in range(RING):
                sp.wait_ge(s_out[h], 16 * (ND // 2))
            if last:
                for b in range(2):
                    sp.wait_ge(s_h2[b], 16 * ND)

        @block.gpsimd
        def _(pool):
            def difference(h, j, v):
                u = (h + j) % 2
                pool.wait_ge(s_cand, v + 1)
                if not is_below(v, 2):
                    pool.wait_ge(s_upd, v - 1)
                nc.gpsimd.tensor_tensor(dif[:, u], fa[:, h, j * Q:(j + 1) * Q, 0:D], cand[:, u], ALU.subtract).then_inc(s_dif, 1)

            def add_to_x(h, j, v):
                rows = slice(j * Q, (j + 1) * Q)
                pool.wait_ge(s_upd, v + 1)
                nc.gpsimd.tensor_tensor(x[:, h, rows], x[:, h, rows], new[:, (h + j) % 2], ALU.add).then_inc(s_new, 1)

            def power(n):
                pool.wait_ge(s_var, n + 1)
                nc.gpsimd.tensor_tensor(stat[:, 2, :], stat[:, 1, :], half[:], ALU.pow).then_inc(s_dev, 1)

            def unit(n, h):
                for j in range(NQ):
                    difference(h, j, NQ * n + j)
                    if last:
                        if j > 0:
                            if j == 1:
                                pool.wait_ge(s_x[h], 2 * in_slot(n, h))
                            add_to_x(h, j - 1, NQ * n + j - 1)
                        elif not is_below(n, 1):
                            add_to_x(1 - h, NQ - 1, NQ * n - 1)
                    if first and j == 2 and not is_from(n, ND - 1):
                        power(n + 1)
                    if last and j == NQ - 1 and not is_below(n, 1):
                        power(n - 1)

            if first or last:
                nc.gpsimd.memset(half[:], -0.5).then_inc(s_half, 1)
                pool.wait_ge(s_half, 1)
            if first:
                power(0)
            pairs(pool, ND, unit)
            if last:
                add_to_x(1, NQ - 1, NV - 1)
                power(ND - 1)

        @block.tensor
        def _(pe):
            def turn(n, h, j, v):
                if j == 0:
                    pe.wait_ge(s_in[h], in_slot(n, h))
                if first:
                    pe.wait_ge(s_f, NP * n + (Q * (j + 1) - 1) // PR + 1)
                if not is_below(v, 2):
                    pe.wait_ge(s_tc, v - 1)
                u = (h + j) % 2
                for k in range(Q):
                    mm = pe.transpose(p_t[u][:, k * P:(k + 1) * P], fa[:, h, j * Q + k, :], m.ident[:])
                mm.then_inc(s_t, 1)

            def gates(u, v):
                if not is_below(v, 2):
                    pe.wait_ge(s_pre, v - 1)
                for b in range(2):
                    pe.matmul(p_g[u][:, 2 * b:2 * b + 2, :].rearrange("p k d -> p (k d)"), lhsT=m.ones3[:],
                              rhs=m.b_gru[:].rearrange("p a d -> p (a d)"), start=True, stop=False, skip_group_check=True)
                pe.wait_ge(s_tc, v + 1)
                for k in range(Q):
                    mm = pe.matmul(p_g[u][:, k, :], lhsT=faT[:, u, k * P:(k + 1) * P], rhs=m.w_gru[:], start=False,
                                   stop=True, skip_group_check=True)
                mm.then_inc(s_g, 1)

            def unit(n, h):
                for j in range(NQ):
                    gates((h + j) % 2, NQ * n + j)
                    if j + 2 < NQ:
                        turn(n, h, j + 2, NQ * n + j + 2)
                    elif not is_from(n, ND - 1):
                        turn(n + 1, 1 - h, j + 2 - NQ, NQ * n + j + 2)

            turn(0, 0, 0, 0)
            turn(0, 0, 1, 1)
            pairs(pe, ND, unit)

        @block.scalar
        def _(act):
            def copy_turned(u, v):
                act.wait_ge(s_t, v + 1)
                nc.scalar.copy(faT[:, u, :], p_t[u][:]).then_inc(s_tc, 1)

            def quad(u, v, more):
                act.wait_ge(s_g, v + 1)
                if not is_below(v, 2):
                    act.wait_ge(s_upd, v - 1)
                nc.scalar.activation(rz[:, u], p_g[u][:, :, 0:2 * D], ACT.Sigmoid).then_inc(s_rz, 1)
                if more:
                    copy_turned(u, v + 2)
                act.wait_ge(s_pre, v + 1)
                nc.scalar.activation(cand[:, u], pre[:, u], ACT.Tanh).then_inc(s_cand, 1)

            def square(n, h, p):
                act.wait_ge(s_cen, NP * n + p + 1)
                cen = fa[:, h, :, 0:D] if first else h2[:]
                nc.scalar.activation(squares(h)[:, p * PR:(p + 1) * PR], cen[:, p * PR:(p + 1) * PR], ACT.Square).then_inc(s_sq, 1)

            def unit(n, h):
                for j in range(NQ):
                    quad((h + j) % 2, NQ * n + j, j + 2 < NQ or not is_from(n, ND - 1))
                    if first and j in (0, 1) and not is_from(n, ND - 1):
                        square(n + 1, 1 - h, 2 * j)
                        square(n + 1, 1 - h, 2 * j + 1)
                    if last and j in (4, 5) and not is_below(n, 1):
                        square(n - 1, 1 - h, 2 * (j - 4))
                        square(n - 1, 1 - h, 2 * (j - 4) + 1)

            act.wait_ge(s_zero, 1)
            nc.scalar.activation(rz[0:1, 0, 0, 0:1], tmp[0:1, 0, 0, 0:1], ACT.Sigmoid).then_inc(s_table, 1)
            act.wait_ge(s_table, 1)
            if first:
                for p in range(NP):
                    square(0, 0, p)
            copy_turned(0, 0)
            copy_turned(1, 1)
            pairs(act, ND, unit)
            if last:
                for p in range(NP):
                    square(ND - 1, 1, p)

        @block.vector
        def _(dve):
            nc.vector.memset(tmp[0:1, 0, 0, 0:1], 0.0).then_inc(s_zero, 1)
            dve.wait_ge(s_zero, 1)

            def norm(op, p, n, h):
                rows = slice(p * PR, (p + 1) * PR)
                cen = (fa[:, h, :, 0:D] if first else h2[:])[:, rows]
                if op == "sum":
                    if p == 0 and first:
                        dve.wait_ge(s_x[h], in_slot(n, h))
                    if p == 0 and last:
                        dve.wait_ge(s_new, NQ * (n + 1))
                        nc.vector.tensor_scalar(sign[:], nt[:, h], -2.0, 1.0, ALU.mult, ALU.add).then_inc(s_sign, 1)
                    nc.vector.tensor_reduce(stat[:, 0, rows], x[:, h, rows], AX.X, ALU.add).then_inc(s_sum, 1)
                if op == "center":
                    if last and not is_below(n, 1) and p % 2 == 0:
                        dve.wait_ge(s_h2[p // 2], 16 * n)
                    dve.wait_ge(s_sum, NP * n + p + 1)
                    nc.vector.scalar_tensor_tensor(out=cen, in0=bc(stat[:, 0, rows], 2, [P, PR, D]), scalar=-1.0 / D,
                                                   in1=x[:, h, rows], op0=ALU.mult, op1=ALU.add).then_inc(s_cen, 1)
                if op == "variance":
                    dve.wait_ge(s_sq, NP * n + p + 1)
                    nc.vector.tensor_reduce(stat[:, 3, rows], squares(h)[:, rows], AX.X, ALU.add).then_inc(s_sq2, 1)
                    if p == NP - 1:
                        dve.wait_ge(s_sq2, NP * (n + 1))
                        nc.vector.tensor_scalar(stat[:, 1, :], stat[:, 3, :], 1.0 / D, EPS, ALU.mult, ALU.add).then_inc(s_var, 1)
                if op == "scale":
                    if p == 0:
                        dve.wait_ge(s_dev, n + 1)
                        if last:
                            dve.wait_ge(s_sign, 2 * n + 1)
                            nc.vector.tensor_tensor(stat[:, 2, :], stat[:, 2, :], sign[:], ALU.mult).then_inc(s_sign, 1)
                            dve.wait_ge(s_sign, 2 * n + 2)
                    nc.vector.scalar_tensor_tensor(out=cen, in0=cen, scalar=0.0, in1=bc(stat[:, 2, rows], 2, [P, PR, D]),
                                                   op0=ALU.max, op1=ALU.mult).then_inc(s_f, 1)

            def pair(op, k, n, h):
                norm(op, 2 * k, n, h)
                norm(op, 2 * k + 1, n, h)

            def norm_beside(j, n, h):
                if first and not is_from(n, ND - 1):
                    if j < 5:
                        pair(*(("center", 1), ("variance", 0), ("variance", 1), ("scale", 0), ("scale", 1))[j], n + 1, 1 - h)
                if first and j >= 4 and not is_from(n, ND - 2):
                    pair(*(("sum", 0), ("sum", 1), ("center", 0))[j - 4], n + 2, h)
                if last and j < 2 and not is_below(n, 2):
                    pair("scale", j, n - 2, h)
                if last and j >= 1 and not is_below(n, 1):
                    pair(*(("sum", 0), ("sum", 1), ("center", 0), ("center", 1), ("variance", 0), ("variance", 1))[j - 1],
                         n - 1, 1 - h)

            def candidate_argument(u, v):
                dve.wait_ge(s_rz, v + 1)
                nc.vector.tensor_tensor(tmp[:, u], rz[:, u, :, 0:D], p_g[u][:, :, 2 * D:3 * D], ALU.mult).then_inc(s_t1, 1)

            def candidate_argument_2(u, v):
                dve.wait_ge(s_t1, v + 1)
                nc.vector.tensor_tensor(pre[:, u], tmp[:, u], p_g[u][:, :, 3 * D:4 * D], ALU.add).then_inc(s_pre, 1)

            def update(h, j, v):
                u = (h + j) % 2
                dve.wait_ge(s_dif, v + 1)
                nc.vector.tensor_tensor(dif[:, u], dif[:, u], rz[:, u, :, D:2 * D], ALU.mult).then_inc(s_dz, 1)
                yield
                if last and not is_below(v, 2):
                    dve.wait_ge(s_new, v - 1)
                dve.wait_ge(s_dz, v + 1)
                to = new[:, u] if last else new[:, h, j * Q:(j + 1) * Q]
                nc.vector.tensor_tensor(to, dif[:, u], cand[:, u], ALU.add).then_inc(s_upd, 1)
                yield

            def unit(n, h):
                for j in range(NQ):
                    v = NQ * n + j
                    if j == 1 and not last and not is_below(n, 2):
                        dve.wait_ge(s_out[h], in_slot(n, h) - 16)
                    candidate_argument((h + j) % 2, v)
                    behind = None
                    if j > 0:
                        behind = update(h, j - 1, v - 1)
                    elif not is_below(n, 1):
                        behind = update(1 - h, NQ - 1, v - 1)
                    if behind:
                        next(behind)
                    candidate_argument_2((h + j) % 2, v)
                    if behind:
                        next(behind)
                    norm_beside(j, n, h)

            if first:
                for op in ("sum", "center", "variance", "scale"):
                    for k in range(2):
                        pair(op, k, 0, 0)
                for op, k in (("sum", 0), ("sum", 1), ("center", 0)):
                    pair(op, k, 1, 1)
            pairs(dve, ND, unit)
            for _ in update(1, NQ - 1, NV - 1):
                pass
            if last:
                for k in range(2):
                    pair("scale", k, ND - 2, 0)
                for op in ("sum", "center", "variance", "scale"):
                    for k in range(2):
                        pair(op, k, ND - 1, 1)
    release(nc, sems)


def attention_logits(nc, m):
    G14 = NP_ // (NG * P)
    sems = []

    def keep(s):
        sems.append(s)
        return s

    with ExitStack() as ctx:
        def sb(name, shape, dt=F32):
            return ctx.enter_context(nc.sbuf_tensor(f"al_{name}", shape, dt))

        def sem(name):
            return keep(nc.alloc_semaphore(f"logits_{name}"))

        idx = sb("idx", [P, RING, 2, U], I32)
        g = sb("g", [P, RING, 2, U, D])
        cen = sb("cen", [P, 2 * U, D])
        sq = sb("sq", [P, 2 * U, D])
        stat = sb("stat", [P, 5, 2 * U])
        hn = sb("hn", [P, RING, 2, U, D])
        dots = sb("dots", [P, 2 * U])
        x = sb("x", [P, RING, G14, D])
        y = sb("y", [P, RING, G14, D])
        s_init = sem("init")
        s_tick = sem("tick")
        s_idx = sem("indices_staged")
        s_g = [sem(f"gathered{k}") for k in range(RING)]
        s_ln = sem("norm_chain")
        s_cen = sem("centered")
        s_sq = sem("squared")
        s_dev = sem("deviation")
        s_h = sem("rows_normed")
        s_hs = [sem(f"rows_stored{k}") for k in range(RING)]
        s_x = [sem(f"x_loaded{k}") for k in range(RING)]
        s_y = sem("x_and_bias")
        s_out = [sem(f"out_stored{k}") for k in range(RING)]
        block = ctx.enter_context(nc.Block())

        @block.sync
        def _(sp):
            xv = m.x.rearrange("(n p k) d -> n p (k d)", p=P, k=G14)

            def load(n, h):
                sp.wait_ge(s_y, n + 1)
                settle(sp, s_tick)
                sp.dma_start(x[:, h].rearrange("p k d -> p (k d)"), xv[bass.ds(n, 1)].rearrange("o p f -> (o p) f")).then_inc(s_x[h], 16)

            def store(n, h):
                sp.wait_ge(s_h, n + 1)
                settle(sp, s_tick)
                sp.dma_start(m.h3[:, bass.ds(tile_base(n), U), :], hn[:, h, 0]).then_inc(s_hs[h], 16)
                sp.wait_ge(s_y, n + 1 + RING)
                settle(sp, s_tick)
                if isinstance(n, int) and n == NG - 1:
                    first = n * P * G14
                    full = (N - first) // G14
                    tail = N - first - full * G14
                    sp.dma_start(m.out[first:first + full * G14].rearrange("(p k) d -> p (k d)", k=G14),
                                 y[0:full, h].rearrange("p k d -> p (k d)")).then_inc(s_out[h], 16)
                    sp.dma_start(m.out[N - tail:N].rearrange("(o k) d -> o (k d)", o=1),
                                 y[full:full + 1, h, 0:tail].rearrange("p k d -> p (k d)")).then_inc(s_out[h], 16)
                else:
                    o = m.out[0:(NG - 1) * P * G14].rearrange("(n p k) d -> n p (k d)", p=P, k=G14)
                    sp.dma_start(o[bass.ds(n, 1)].rearrange("o p f -> (o p) f"), y[:, h].rearrange("p k d -> p (k d)")).then_inc(s_out[h], 16)

            lagged(sp, NG, load, store)
            for h in range(RING):
                sp.wait_ge(s_hs[h], 16 * (NG // 2))
                sp.wait_ge(s_out[h], 16 * (NG // 2 + h))

        @block.gpsimd
        def _(pool):
            limit = pool.to_reg(N - 1)

            def fetch(n, h):
                pool.wait_ge(s_idx, n + 1)
                settle(pool, s_tick)
                for a in range(2):
                    for k in range(U):
                        nc.gpsimd.indirect_dma_start(
                            out=g[:, h, a, k, :], out_offset=None, in_=m.x,
                            in_offset=bass.IndirectOffsetOnAxis(ap=idx[:, h, a, k:k + 1], axis=0),
                            bounds_check=limit, oob_is_err=False).then_inc(s_g[h], 16)

            with pool.Fori(0, NG // 2) as i:
                for h in range(2):
                    fetch(2 * i + h, h)

        @block.scalar
        def _(act):
            with act.Fori(0, NG // 2) as i:
                for h in range(2):
                    n = 2 * i + h
                    act.wait_ge(s_cen, n + 1)
                    nc.scalar.activation(sq[:], cen[:], ACT.Square).then_inc(s_sq, 1)
                    act.wait_ge(s_dev, 2 * n + 1)
                    nc.scalar.activation(stat[:, 2, :], stat[:, 1, :], ACT.Sqrt, bias=m.eps[:, 0:1], scale=1.0 / D).then_inc(s_dev, 1)

        @block.vector
        def _(dve):
            nc.vector.memset(g[:], 0.0).then_inc(s_init, 1)
            dve.wait_ge(s_init, 1)
            dve.sem_inc(s_y, RING)
            for n in range(RING):
                nc.vector.tensor_copy(idx[:, n, 0, :], m.src_i[:, FRONT + tile_base(n):FRONT + tile_base(n) + U])
                nc.vector.tensor_copy(idx[:, n, 1, :], m.dst_i[:, FRONT + tile_base(n):FRONT + tile_base(n) + U]).then_inc(s_idx, 1)
            def group(n, h):
                dve.wait_ge(s_g[h], 2 * U * (8 * (n - h) + 16))
                ch = Chain(dve, s_ln, 6 * n)
                rows = g[:, h].rearrange("p a k d -> p (a k) d")
                ch.then(nc.vector.tensor_reduce(stat[:, 0, :], rows, AX.X, ALU.add))
                nc.vector.scalar_tensor_tensor(out=cen[:], in0=bc(stat[:, 0, :], 2, [P, 2 * U, D]), scalar=-1.0 / D,
                                               in1=rows, op0=ALU.mult, op1=ALU.add).then_inc(s_cen, 1)
                dve.wait_ge(s_x[h], 8 * (n - h) + 16)
                if not is_below(n, 2):
                    dve.wait_ge(s_out[h], 8 * (n - h))
                nc.vector.tensor_tensor(y[:, h], x[:, h], bc(m.bias3[:], 1, [P, G14, D]), ALU.add).then_inc(s_y, 1)
                dve.wait_ge(s_sq, n + 1)
                nc.vector.tensor_copy(idx[:, h, 0, :], m.src_i[:, bass.ds(FRONT + tile_base(n + 2), U)])
                nc.vector.tensor_copy(idx[:, h, 1, :], m.dst_i[:, bass.ds(FRONT + tile_base(n + 2), U)]).then_inc(s_idx, 1)
                nc.vector.tensor_reduce(stat[:, 1, :], sq[:], AX.X, ALU.add).then_inc(s_dev, 1)
                dve.wait_ge(s_dev, 2 * n + 2)
                ch.then(nc.vector.reciprocal(stat[:, 3, :], stat[:, 2, :]))
                if not is_below(n, 2):
                    dve.wait_ge(s_hs[h], 8 * (n - h))
                both = hn[:, h].rearrange("p a k d -> p (a k) d")
                nc.vector.scalar_tensor_tensor(out=both, in0=cen[:], scalar=0.0, in1=bc(stat[:, 3, :], 2, [P, 2 * U, D]),
                                               op0=ALU.max, op1=ALU.mult).then_inc(s_h, 1)
                dve.wait_ge(s_h, n + 1)
                nc.vector.tensor_tensor(cen[:, 0:U], hn[:, h, 0], bc(m.wl[:], 1, [P, U, D]), ALU.mult)
                ch.then(nc.vector.tensor_tensor(cen[:, U:2 * U], hn[:, h, 1], bc(m.wr[:], 1, [P, U, D]), ALU.mult))
                ch.then(nc.vector.tensor_reduce(dots[:], cen[:], AX.X, ALU.add))
                ch.then(nc.vector.tensor_tensor(stat[:, 4, 0:U], dots[:, 0:U], dots[:, U:2 * U], ALU.add))
                ch.then(nc.vector.scalar_tensor_tensor(out=m.e_t[:, bass.ds(tile_base(n), U)], in0=stat[:, 4, 0:U], scalar=0.2,
                                               in1=stat[:, 4, 0:U], op0=ALU.mult, op1=ALU.max))

            pairs(dve, NG, group)
    release(nc, sems)


def attention_weights(nc, m):
    sems = []

    def keep(s):
        sems.append(s)
        return s

    with ExitStack() as ctx:
        def sb(name, shape, dt=F32):
            return ctx.enter_context(nc.sbuf_tensor(f"aw_{name}", shape, dt))

        def ps(name, shape):
            return ctx.enter_context(nc.psum_tensor(f"aw_{name}", shape, F32))

        e = sb("e", [R, CH, P])
        gate_f = sb("gate_f", [R, CH, P])
        gate_b = sb("gate_b", [R, CH, P])
        fwd = sb("fwd", [R, CH, P])
        bwd = sb("bwd", [R, CH, P])
        thru = sb("thru", [R, 2, CH])
        ends = sb("ends", [1, 4, T])
        run = sb("run", [1, 2, T + 1])
        carry = sb("carry", [R, 2, CH])
        p_e = ps("p_e", [R, CH * P])
        p_ends = [ps(f"p_ends{k}", [1, 512]) for k in range(4)]
        p_carry = ps("p_carry", [R, 2 * CH])
        p_back = ps("p_back", [P, 512])
        s_c = keep(nc.alloc_semaphore("weights_chain"))
        s_t = keep(nc.alloc_semaphore("weights_turned"))
        s_d = keep(nc.alloc_semaphore("weights_rows_ready"))
        s_x = keep(nc.alloc_semaphore("weights_exp"))
        block = ctx.enter_context(nc.Block())

        @block.tensor
        def _(pe):
            for c in range(CH):
                mm = pe.transpose(p_e[:, c * P:(c + 1) * P], m.e_t[:, c * R:(c + 1) * R], m.ident[:])
            mm.then_inc(s_t, 1)
            pe.wait_ge(s_d, 1)
            for c in range(CH):
                cols = slice(c * R, (c + 1) * R)
                pe.transpose(p_ends[0][:, cols], fwd[:, c, P - 1:P], m.ident[0:R, 0:R])
                pe.transpose(p_ends[1][:, cols], bwd[:, c, 0:1], m.ident[0:R, 0:R])
                pe.transpose(p_ends[2][:, cols], thru[:, 0, c:c + 1], m.ident[0:R, 0:R])
                mm = pe.transpose(p_ends[3][:, cols], thru[:, 1, c:c + 1], m.ident[0:R, 0:R])
            mm.then_inc(s_t, 1)
            pe.wait_ge(s_d, 2)
            for c in range(CH):
                pe.transpose(p_carry[:, c:c + 1], run[:, 0, c * R:(c + 1) * R], m.ident[0:1, 0:1])
                mm = pe.transpose(p_carry[:, CH + c:CH + c + 1], run[:, 1, c * R + 1:(c + 1) * R + 1], m.ident[0:1, 0:1])
            mm.then_inc(s_t, 1)
            pe.wait_ge(s_x, 1)
            for c in range(CH):
                mm = pe.transpose(p_back[:, c * R:(c + 1) * R], e[:, c, :], m.ident[0:R, 0:R])
            mm.then_inc(s_t, 1)

        @block.scalar
        def _(act):
            act.wait_ge(s_d, 3)
            nc.scalar.activation(e[:], bwd[:], ACT.Exp).then_inc(s_x, 1)

        @block.vector
        def _(dve):
            ch = Chain(dve, s_c, 0)
            dst = m.dst_f
            nc.vector.tensor_tensor(gate_f[:, :, 1:P], dst[:, :, 1:P], dst[:, :, 0:P - 1], ALU.is_equal)
            nc.vector.tensor_tensor(gate_f[:, :, 0], dst[:, :, 0], m.before[:], ALU.is_equal)
            nc.vector.tensor_tensor(gate_b[:, :, 0:P - 1], dst[:, :, 1:P], dst[:, :, 0:P - 1], ALU.is_equal)
            nc.vector.tensor_tensor(gate_b[:, :, P - 1], dst[:, :, P - 1], m.after[:], ALU.is_equal)
            nc.vector.tensor_tensor(thru[:, 0, :], dst[:, :, P - 1], m.before[:], ALU.is_equal)
            ch.then(nc.vector.tensor_tensor(thru[:, 1, :], dst[:, :, 0], m.after[:], ALU.is_equal))
            for t in (gate_f, gate_b, thru):
                ins_ = nc.vector.tensor_scalar(t[:], t[:], -1.0, BIG, ALU.add, ALU.mult)
            ch.then(ins_)
            nc.vector.memset(run[:], -BIG)
            dve.wait_ge(s_t, 1)
            ch.then(nc.vector.tensor_copy(e[:].rearrange("r c p -> r (c p)"), p_e[:]))
            for c in range(CH):
                nc.vector.tensor_tensor_scan(fwd[:, c, :], gate_f[:, c, :], e[:, c, :], -BIG, ALU.add, ALU.max)
                ins_ = nc.vector.tensor_tensor_scan(bwd[:, c, ::-1], gate_b[:, c, ::-1], e[:, c, ::-1], -BIG, ALU.add, ALU.max)
            ins_.then_inc(s_d, 1)
            dve.wait_ge(s_t, 2)
            for k in range(4):
                ins_ = nc.vector.tensor_copy(ends[:, k, :], p_ends[k][:, 0:T])
            ch.then(ins_)
            nc.vector.tensor_tensor_scan(run[:, 0, 1:T + 1], ends[:, 2, :], ends[:, 0, :], -BIG, ALU.add, ALU.max)
            nc.vector.tensor_tensor_scan(run[:, 1, T - 1::-1], ends[:, 3, ::-1], ends[:, 1, ::-1], -BIG, ALU.add, ALU.max).then_inc(s_d, 1)
            dve.wait_ge(s_t, 3)
            ch.then(nc.vector.tensor_copy(carry[:].rearrange("r a c -> r (a c)"), p_carry[:]))
            nc.vector.tensor_tensor(gate_f[:], dst[:], bc(m.before[:], 2, [R, CH, P]), ALU.is_equal)
            ch.then(nc.vector.tensor_tensor(gate_b[:], dst[:], bc(m.after[:], 2, [R, CH, P]), ALU.is_equal))
            nc.vector.tensor_scalar(gate_f[:], gate_f[:], -1.0, BIG, ALU.add, ALU.mult)
            ch.then(nc.vector.tensor_scalar(gate_b[:], gate_b[:], -1.0, BIG, ALU.add, ALU.mult))
            nc.vector.tensor_tensor(gate_f[:], gate_f[:], bc(carry[:, 0, :], 2, [R, CH, P]), ALU.add)
            ch.then(nc.vector.tensor_tensor(gate_b[:], gate_b[:], bc(carry[:, 1, :], 2, [R, CH, P]), ALU.add))
            nc.vector.tensor_tensor(fwd[:], fwd[:], gate_f[:], ALU.max)
            ch.then(nc.vector.tensor_tensor(bwd[:], bwd[:], gate_b[:], ALU.max))
            ch.then(nc.vector.tensor_tensor(fwd[:], fwd[:], bwd[:], ALU.max))
            nc.vector.tensor_tensor(bwd[:], e[:], fwd[:], ALU.subtract).then_inc(s_d, 1)
            dve.wait_ge(s_t, 4)
            ch.then(nc.vector.tensor_copy(m.e_t[:], p_back[:, 0:T]))
    release(nc, sems)


def build(nc, ins, out):
    with ExitStack() as ctx:
        m = allocate(nc, ctx, ins, out)
        halves = m.fa.rearrange("n (a d) -> (n a) d", a=2)
        set_up(nc, m)
        edge_round(nc, m, "sum", ins["x"], m.x)
        edge_round(nc, m, "first", m.x, halves)
        dense_step(nc, m, 0)
        for step in (1, 2, 3):
            edge_round(nc, m, "step", halves, halves)
            dense_step(nc, m, step)
        edge_round(nc, m, "typed", m.h2, m.x)
        attention_logits(nc, m)
        attention_weights(nc, m)
        edge_round(nc, m, "attend", None, out)


INPUTS = ["x", "src", "dst", "edge_attr_32", "edge_type_3", "edge_type_4", "edge_weight", "node_type_2",
          "L1_gnn_W", "L1_gnn_b", "L1_gnn_w_ih", "L1_gnn_w_hh", "L1_gnn_b_ih", "L1_gnn_b_hh",
          "L2_gnn_W_node", "L2_gnn_W_msg", "L3_gnn_W", "L3_gnn_attn_l", "L3_gnn_attn_r", "L3_gnn_bias"]


def kernel(**inputs):
    import numpy as _np
    import concourse.bacc as _bacc
    from concourse.bass_utils import run_bass_kernel_spmd as _run

    nc = _bacc.Bacc("TRN2", target_bir_lowering=False, num_devices=1)
    arrays, aps = {}, {}
    for name in INPUTS:
        a = _np.ascontiguousarray(inputs[name])
        arrays[f"in_{name}"] = a
        aps[name] = nc.dram_tensor(f"in_{name}", a.shape, mybir.dt.from_np(a.dtype), kind="ExternalInput").ap()
    out = nc.dram_tensor("out_0", (N, D), F32, kind="ExternalOutput").ap()
    build(nc, aps, out)
    r = _run(nc, [arrays], core_ids=[0])
    return r.results[0]["out_0"]
```
